# Optimizing a Trainium2 kernel written in Bass

```python
import numpy as np
import jax
import jax.numpy as jnp

def _softmax(x, axis=-1):
    return jax.nn.softmax(x, axis=axis)

def _gelu(x):
    return jax.nn.gelu(x, approximate=True)

def _silu(x):
    return jax.nn.silu(x)

def _sigmoid(x):
    return jax.nn.sigmoid(x)

def _layernorm(x, axis=-1, eps=1e-05):
    m = jnp.mean(x, axis=axis, keepdims=True)
    v = jnp.var(x, axis=axis, keepdims=True)
    return (x - m) / jnp.sqrt(v + eps)

def _scatter_add(tgt, idx, src, axis=0):
    return tgt.at[idx].add(src)

def _segment_sum(src, seg, n):
    return jax.ops.segment_sum(src, seg, n)
kernel_name = 'mk_prb_d1_jaxref_r4_eceb4e'

def setup_inputs(seed: int=0):
    np.random.seed(seed)
    _w = jnp.asarray

    def _L0_attn_setup():
        import jax, jax.numpy as jnp
        import numpy as np
        import math
        B, T, C = (2, 512, 256)
        H, L = (16, 64)
        DH = C // H
        DHE = DH // 2
        THETA = 10000.0

        def _rope_cache(t, dim):
            inv_freq = 1.0 / THETA ** (jnp.arange(0, dim, 2, dtype=jnp.float32) / dim)
            freqs = jnp.arange(t, dtype=jnp.float32)[:, None] * inv_freq[None, :]
            emb = jnp.concatenate((freqs, freqs), axis=-1)
            return (jnp.cos(emb), jnp.sin(emb))

        def _apply_rope(x, cos, sin):
            x1 = x[..., 0::2]
            x2 = x[..., 1::2]
            rot = jnp.stack((-x2, x1), axis=-1).reshape(x.shape)
            return x * cos[None, None] + rot * sin[None, None]
        key = jax.random.key(seed)
        ks = jax.random.split(key, 10)
        s = 0.02
        return {'x': jax.random.normal(ks[0], (B, T, C), jnp.float32), 'Wq_down': jax.random.normal(ks[1], (C, H * L), jnp.float32) * s, 'Wk_down': jax.random.normal(ks[2], (C, H * L), jnp.float32) * s, 'Wv_down': jax.random.normal(ks[3], (C, H * L), jnp.float32) * s, 'Wq_up_c': jax.random.normal(ks[4], (L, DHE), jnp.float32) * s, 'Wq_up_e': jax.random.normal(ks[5], (L, DHE), jnp.float32) * s, 'Wk_up_c': jax.random.normal(ks[6], (L, DHE), jnp.float32) * s, 'Wk_up_e': jax.random.normal(ks[7], (L, DHE), jnp.float32) * s, 'Wv_up': jax.random.normal(ks[8], (L, DH), jnp.float32) * s, 'Wc': jax.random.normal(ks[9], (C, C), jnp.float32) * s}
    _L0_attn_in = _L0_attn_setup()

    def _L0_ffn_setup():
        import jax, jax.numpy as jnp
        import numpy as np
        EPS = 1e-06
        LN_EPS = 1e-05

        def _absmean_core(W):
            gamma = jnp.mean(jnp.abs(W)) + EPS
            Ws = W / gamma
            Wq = jnp.sign(Ws) * jnp.minimum(jnp.round(jnp.abs(Ws)), 1.0)
            return (Wq, gamma)

        @jax.custom_vjp
        def absmean(W):
            return _absmean_core(W)[0]

        def _absmean_fwd(W):
            Wq, gamma = _absmean_core(W)
            return (Wq, gamma)

        def _absmean_bwd(gamma, g):
            return (g / gamma,)
        absmean.defvjp(_absmean_fwd, _absmean_bwd)

        def layernorm(x, w, b, eps=LN_EPS):
            mu = jnp.mean(x, axis=-1, keepdims=True)
            var = jnp.mean((x - mu) ** 2, axis=-1, keepdims=True)
            return (x - mu) * jax.lax.rsqrt(var + eps) * w + b
        key = jax.random.key(seed)
        k1, k2, k3 = jax.random.split(key, 3)
        d, h = (256, 1024)
        B, T = (8, 512)
        return {'x': jax.random.normal(k1, (B, T, d), jnp.float32), 'W_fc': jax.random.normal(k2, (h, d), jnp.float32), 'ln_w': jnp.ones((h,), jnp.float32), 'ln_b': jnp.zeros((h,), jnp.float32), 'W_proj': jax.random.normal(k3, (d, h), jnp.float32)}
    _L0_ffn_in = _L0_ffn_setup()
    _d = {'L0_attn_x': _L0_attn_in['x'], 'L0_attn_Wq_down': _L0_attn_in['Wq_down'], 'L0_attn_Wk_down': _L0_attn_in['Wk_down'], 'L0_attn_Wv_down': _L0_attn_in['Wv_down'], 'L0_attn_Wq_up_c': _L0_attn_in['Wq_up_c'], 'L0_attn_Wq_up_e': _L0_attn_in['Wq_up_e'], 'L0_attn_Wk_up_c': _L0_attn_in['Wk_up_c'], 'L0_attn_Wk_up_e': _L0_attn_in['Wk_up_e'], 'L0_attn_Wv_up': _L0_attn_in['Wv_up'], 'L0_attn_Wc': _L0_attn_in['Wc'], 'L0_ffn_W_fc': _L0_ffn_in['W_fc'], 'L0_ffn_ln_w': _L0_ffn_in['ln_w'], 'L0_ffn_ln_b': _L0_ffn_in['ln_b'], 'L0_ffn_W_proj': _L0_ffn_in['W_proj']}
    _x0 = _d['L0_attn_x']
    _d['L0_attn_x'] = jax.random.normal(jax.random.fold_in(jax.random.key(seed), 1), (4, 2048, 256), dtype=_x0.dtype)
    del _x0
    return _d

def reference(L0_attn_x, L0_attn_Wq_down, L0_attn_Wk_down, L0_attn_Wv_down, L0_attn_Wq_up_c, L0_attn_Wq_up_e, L0_attn_Wk_up_c, L0_attn_Wk_up_e, L0_attn_Wv_up, L0_attn_Wc, L0_ffn_W_fc, L0_ffn_ln_w, L0_ffn_ln_b, L0_ffn_W_proj):

    def _L0_attn_ref(x, Wq_down, Wk_down, Wv_down, Wq_up_c, Wq_up_e, Wk_up_c, Wk_up_e, Wv_up, Wc):
        import jax, jax.numpy as jnp
        import numpy as np
        import math
        B, T, C = (2, 512, 256)
        H, L = (16, 64)
        DH = C // H
        DHE = DH // 2
        THETA = 10000.0

        def _rope_cache(t, dim):
            inv_freq = 1.0 / THETA ** (jnp.arange(0, dim, 2, dtype=jnp.float32) / dim)
            freqs = jnp.arange(t, dtype=jnp.float32)[:, None] * inv_freq[None, :]
            emb = jnp.concatenate((freqs, freqs), axis=-1)
            return (jnp.cos(emb), jnp.sin(emb))

        def _apply_rope(x, cos, sin):
            x1 = x[..., 0::2]
            x2 = x[..., 1::2]
            rot = jnp.stack((-x2, x1), axis=-1).reshape(x.shape)
            return x * cos[None, None] + rot * sin[None, None]
        b, t, c = x.shape
        q_lat = (x @ Wq_down).reshape(b, t, H, L)
        k_lat = (x @ Wk_down).reshape(b, t, H, L)
        v_lat = (x @ Wv_down).reshape(b, t, H, L)
        q_c = jnp.einsum('bthl,ld->bhtd', q_lat, Wq_up_c)
        q_e = jnp.einsum('bthl,ld->bhtd', q_lat, Wq_up_e)
        k_c = jnp.einsum('bthl,ld->bhtd', k_lat, Wk_up_c)
        k_e = jnp.einsum('bthl,ld->bhtd', k_lat, Wk_up_e)
        v = jnp.einsum('bthl,ld->bhtd', v_lat, Wv_up)
        cos, sin = _rope_cache(t, DHE)
        q = jnp.concatenate([q_c, _apply_rope(q_e, cos, sin)], axis=-1)
        k = jnp.concatenate([k_c, _apply_rope(k_e, cos, sin)], axis=-1)
        scale = 1.0 / math.sqrt(DH)
        scores = jnp.einsum('bhqd,bhkd->bhqk', q, k) * scale
        causal = jnp.tril(jnp.ones((t, t), dtype=bool))
        scores = jnp.where(causal[None, None], scores, -jnp.inf)
        att = jax.nn.softmax(scores, axis=-1)
        y = jnp.einsum('bhqk,bhkd->bhqd', att, v)
        y = y.transpose(0, 2, 1, 3).reshape(b, t, c)
        return y @ Wc

    def _L0_ffn_ref(x, W_fc, ln_w, ln_b, W_proj):
        import jax, jax.numpy as jnp
        import numpy as np
        EPS = 1e-06
        LN_EPS = 1e-05

        def _absmean_core(W):
            gamma = jnp.mean(jnp.abs(W)) + EPS
            Ws = W / gamma
            Wq = jnp.sign(Ws) * jnp.minimum(jnp.round(jnp.abs(Ws)), 1.0)
            return (Wq, gamma)

        @jax.custom_vjp
        def absmean(W):
            return _absmean_core(W)[0]

        def _absmean_fwd(W):
            Wq, gamma = _absmean_core(W)
            return (Wq, gamma)

        def _absmean_bwd(gamma, g):
            return (g / gamma,)
        absmean.defvjp(_absmean_fwd, _absmean_bwd)

        def layernorm(x, w, b, eps=LN_EPS):
            mu = jnp.mean(x, axis=-1, keepdims=True)
            var = jnp.mean((x - mu) ** 2, axis=-1, keepdims=True)
            return (x - mu) * jax.lax.rsqrt(var + eps) * w + b
        h = jnp.einsum('btd,hd->bth', x, absmean(W_fc))
        h = jax.nn.gelu(h, approximate=False)
        h = layernorm(h, ln_w, ln_b)
        return jnp.einsum('bth,dh->btd', h, absmean(W_proj))
    x = L0_attn_x
    xn = _layernorm(x, axis=-1)
    x = x + _L0_attn_ref(xn, L0_attn_Wq_down, L0_attn_Wk_down, L0_attn_Wv_down, L0_attn_Wq_up_c, L0_attn_Wq_up_e, L0_attn_Wk_up_c, L0_attn_Wk_up_e, L0_attn_Wv_up, L0_attn_Wc) + _L0_ffn_ref(xn, L0_ffn_W_fc, L0_ffn_ln_w, L0_ffn_ln_b, L0_ffn_W_proj)
    return x

_drawn_inputs = setup_inputs


def setup_inputs(seed=0):
    import zlib

    import numpy as np

    out = dict(_drawn_inputs(seed))
    spreads = {'L0_ffn_ln_w': (1.0, 0.2), 'L0_ffn_ln_b': (0.0, 0.1)}
    factors = {'L0_attn_Wq_down': 8.0,
     'L0_attn_Wk_down': 8.0,
     'L0_attn_Wv_down': 8.0,
     'L0_attn_Wq_up_c': 8.0,
     'L0_attn_Wq_up_e': 8.0,
     'L0_attn_Wk_up_c': 8.0,
     'L0_attn_Wk_up_e': 8.0,
     'L0_attn_Wv_up': 8.0,
     'L0_attn_Wc': 8.0}
    for name, (base, spread) in spreads.items():
        noise = np.random.default_rng([zlib.crc32(name.encode()), seed]).standard_normal(out[name].shape)
        drawn = base * np.exp(spread * noise) if base else spread * noise
        out[name] = jnp.asarray(drawn.astype(out[name].dtype))
    for name, factor in factors.items():
        out[name] = (out[name] * factor).astype(out[name].dtype)
    return out
```

```python
import concourse.bass as bass
from concourse import mybir
from contextlib import ExitStack

fp32 = mybir.dt.float32
fp16 = mybir.dt.float16
bf16 = mybir.dt.bfloat16
ALU = mybir.AluOpType
ACT = mybir.ActivationFunctionType
AX = mybir.AxisListType

P = 128
B, T, C = 4, 2048, 256
H, L, DH = 16, 64, 16
HID = 1024
CC = C // P
HC = HID // P
CH = 512
NCH = B * T // CH
SUB = CH // P
TC = T // CH
G = 4
NQ = B * H // G
QB = H // G
PARTS = 3
LN_EPS = 1e-5
W_EPS = 1e-6


def grant(eng, *credits):
    for sem, value in credits:
        eng.nop().then_inc(sem, value)


class Steps:

    def __init__(self, eng, sem, per):
        self.eng, self.sem, self.per, self.n, self.base = eng, sem, per, 0, 0

    def start(self, turn):
        self.base, self.n = turn * self.per, 0

    def done(self, instruction):
        self.n += 1
        instruction.then_inc(self.sem, 1)

    def wait(self):
        self.eng.wait_ge(self.sem, self.base + self.n)

    def end(self):
        assert self.n == self.per, (self.n, self.per)


def wait_apart(eng, spare, sem, count, past, value):
    if not isinstance(count, int):
        count = eng.snap(count)
    eng.reg_mov(spare, count)
    eng.wait_ge(past, value)
    eng.wait_ge(sem, count)


def make_weights(nc, io, w):
    with ExitStack() as ctx:
        def sb(name, shape, dt=fp32):
            return ctx.enter_context(nc.sbuf_tensor(name, shape, dt))

        def sem(name):
            return ctx.enter_context(nc.semaphore(name))

        down = [sb(f"w_down{m}", [P, CC, H * L]) for m in range(3)]
        downT = sb("w_downT", [P, H // 2, C])
        up = [sb(f"w_up{m}", [P, 16]) for m in range(3)]
        upd = [sb(f"w_upd{m}", [P, 2, 24 if m < 2 else 16]) for m in range(3)]
        fc = sb("w_fc_raw", [P, HC, C])
        pj = sb("w_proj_raw", [P, CC, HID])
        fneg = sb("w_fneg", [P, HC, C], fp16)
        fter = sb("w_fter", [P, HC, C], fp16)
        pneg = sb("w_pneg", [P, CC, HID], fp16)
        pter = sb("w_pter", [P, CC, HID], fp16)
        lnw = sb("w_lnw", [P, HC])
        lnb = sb("w_lnb", [P, HC])
        wb = sb("w_bias_rows", [P, HC, C])
        asum = sb("w_asum", [P, 2])
        thr = sb("w_thr", [P, 2])
        nthr = sb("w_nthr", [P, 2])
        ones = sb("w_ones", [P, P])
        idh = sb("w_idh", [P, P], fp16)
        tp = [ctx.enter_context(nc.psum_tensor(f"wp_t{i}", [P, CH], fp32)) for i in range(2)]
        fo = [ctx.enter_context(nc.psum_tensor(f"wp_f{i}", [P, CH], fp32)) for i in range(2)]
        th = [ctx.enter_context(nc.psum_tensor(f"wp_h{i}", [P, 1024], fp16)) for i in range(2)]
        sm = ctx.enter_context(nc.psum_tensor("wp_s", [P, CH], fp32))

        s_down = [sem(f"w_down_loaded{m}") for m in range(3)]
        s_up = sem("w_up_loaded")
        s_ff = sem("w_ff_loaded")
        s_misc = sem("w_misc_loaded")
        s_const = sem("w_const_ready")
        s_pool = sem("w_pool_steps")
        s_dve = sem("w_dve_steps")
        s_upd = sem("w_upd_ready")
        s_asum = sem("w_asum_ready")
        s_sum = sem("w_sum_ready")
        s_ter = sem("w_ternary_ready")
        s_tp = sem("w_transposed")
        s_tpr = sem("w_transposed_read")
        s_fo = sem("w_folded")
        s_for = sem("w_folded_read")
        s_th = sem("w_ternary_transposed")
        s_thr = sem("w_ternary_transposed_read")
        s_cs = sem("w_column_sums")
        block = ctx.enter_context(nc.Block())

        ups = [("Wq_up_c", "Wq_up_e"), ("Wk_up_c", "Wk_up_e"), ("Wv_up",)]

        @block.sync
        def _(sp):
            sp.dma_start(fc[:, :, :], io["W_fc"].rearrange("(p a) c -> p a c", a=HC)).then_inc(s_ff, 16)
            sp.dma_start(pj[:, :, :], io["W_proj"].rearrange("(a p) h -> p a h", p=P)).then_inc(s_ff, 16)
            for m, names in enumerate(ups):
                for half in range(2):
                    for k, name in enumerate(names):
                        wide = io[name].shape[1]
                        sp.dma_start(up[m][64 * half:64 * half + 64, k * wide:(k + 1) * wide],
                                     io[name]).then_inc(s_up, 16)
            for m, name in enumerate(("Wq_down", "Wk_down", "Wv_down")):
                sp.dma_start(down[m][:, :, :], io[name].rearrange("(a p) n -> p a n", p=P)).then_inc(s_down[m], 16)
            sp.dma_start(lnw[:, :], io["ln_w"].rearrange("(p a) -> p a", a=HC)).then_inc(s_misc, 16)
            sp.dma_start(lnb[:, :], io["ln_b"].rearrange("(p a) -> p a", a=HC)).then_inc(s_misc, 16)
            sp.dma_start(w["cos"][:, :], io["cos"]).then_inc(s_misc, 16)
            sp.dma_start(w["sin"][:, :], io["sin"]).then_inc(s_misc, 16)
            sp.wait_ge(s_misc, 64)

        @block.gpsimd
        def _(pool):
            pool.memset(w["ident"][:, :], 0.0).then_inc(s_pool, 1)
            pool.memset(idh[:, :], 0.0).then_inc(s_pool, 1)
            pool.wait_ge(s_pool, 2)
            for m in (w["ident"], idh):
                pool.affine_select(out=m[:, :], in_=m[:, :], compare_op=ALU.not_equal, fill=1.0, base=0,
                                   pattern=[[-1, P]], channel_multiplier=1).then_inc(s_const, 1)
            pool.memset(ones[:, :], 1.0).then_inc(s_const, 1)
            pool.memset(w["mhalf"][:, :], -0.5).then_inc(s_const, 1)
            pool.memset(w["mean_col"][:, :], 1.0 / HID).then_inc(s_const, 1)
            pool.memset(w["WP"][:, :, C:C + 1], 1.0 / HID).then_inc(s_const, 1)

        @block.vector
        def _(dve):
            me = Steps(dve, s_dve, 0)
            for m in range(3):
                me.done(dve.memset(upd[m][:, :, :], 0.0))
            dve.wait_ge(s_ff, 32)
            dve.tensor_reduce(out=asum[:, 0:1], in_=fc[:, :, :], axis=AX.XY, op=ALU.add,
                              apply_absolute_value=True).then_inc(s_asum, 1)
            dve.tensor_reduce(out=asum[:, 1:2], in_=pj[:, :, :], axis=AX.XY, op=ALU.add,
                              apply_absolute_value=True).then_inc(s_asum, 1)
            dve.wait_ge(s_up, 16 * 10)
            me.wait()
            for m in range(3):
                for half in range(2):
                    r = slice(64 * half, 64 * half + 64)
                    if m == 2:
                        dve.tensor_copy(upd[m][r, half, :], up[m][r, :]).then_inc(s_upd, 1)
                        continue
                    eo = up[m][r, 8:16].rearrange("p (d g) -> p g d", g=2)
                    dve.tensor_copy(upd[m][r, half, 0:8], up[m][r, 0:8]).then_inc(s_upd, 1)
                    dve.tensor_copy(upd[m][r, half, 8:16].rearrange("p (g d) -> p g d", g=2), eo).then_inc(s_upd, 1)
                    dve.tensor_scalar(upd[m][r, half, 16:20], eo[:, 1, :], -1.0, None, ALU.mult).then_inc(s_upd, 1)
                    dve.tensor_copy(upd[m][r, half, 20:24], eo[:, 0, :]).then_inc(s_upd, 1)
            dve.wait_ge(s_sum, 1)
            me.done(dve.tensor_scalar(thr[:, :], sm[:, 0:2], 0.5 / (HID * C), 0.5 * W_EPS, ALU.mult, ALU.add))
            me.wait()
            me.done(dve.tensor_scalar(nthr[:, :], thr[:, :], -1.0, None, ALU.mult))
            me.wait()
            for n, (raw, neg, ter) in enumerate(((fc, fneg, fter), (pj, pneg, pter))):
                flat = [t[:, :, :].rearrange("p a b -> p (a b)") for t in (raw, neg, ter)]
                me.done(dve.tensor_scalar(flat[1], flat[0], nthr[:, n:n + 1], None, ALU.is_lt))
                me.wait()
                dve.scalar_tensor_tensor(out=flat[2], in0=flat[0], scalar=thr[:, n:n + 1], in1=flat[1],
                                         op0=ALU.is_gt, op1=ALU.subtract).then_inc(s_ter, 1)
            dve.wait_ge(s_misc, 64)
            for n in range(2):
                dve.wait_ge(s_th, n + 1)
                dve.tensor_copy(w["WF"][:, n, :], th[n % 2][:, :]).then_inc(s_thr, 1)
            for n in range(2):
                dve.wait_ge(s_th, 3 + n)
                for k in range(4):
                    hc = 4 * n + k
                    src = th[n % 2][:, k * C:(k + 1) * C]
                    me.done(dve.tensor_scalar(w["WP"][:, hc, 0:C], src, lnw[:, hc:hc + 1], None, ALU.mult))
                    i = dve.tensor_scalar(wb[:, hc, :], src, lnb[:, hc:hc + 1], None, ALU.mult)
                i.then_inc(s_thr, 1)
            dve.wait_ge(s_cs, 1)
            dve.tensor_scalar(w["NB"][:, :], sm[:, 0:C], -1.0, None, ALU.mult)
            dve.tensor_copy(w["CB"][:, :], sm[:, C:2 * C]).then_inc(s_cs, 1)

        @block.scalar
        def _(act):
            for m in range(3):
                for k in range(4):
                    act.wait_ge(s_tp, 4 * m + k + 1)
                    if m and k == 0:
                        act.wait_ge(s_fo, 2 * m)
                    act.activation(downT[:, 2 * k:2 * k + 2, :],
                                   tp[k % 2][:, :].rearrange("p (a c) -> p a c", a=2), ACT.Copy).then_inc(s_tpr, 1)
                for cc in range(CC):
                    act.wait_ge(s_fo, 2 * m + cc + 1)
                    if m == 2:
                        act.activation(w["WV"][:, cc, :], fo[cc][:, 0:C], ACT.Copy).then_inc(s_for, 1)
                        continue
                    scale = float(DH) ** -0.5 if m == 0 else 1.0
                    base = m * 3 * P
                    src = fo[cc][:, 0:H * 24].rearrange("p (h e) -> p h e", e=24)
                    act.activation(w["WQK"][:, cc, base:base + P].rearrange("p (h e) -> p h e", e=8),
                                   src[:, :, 0:8], ACT.Copy, scale=scale)
                    for g in range(4):
                        i = act.activation(
                            w["WQK"][:, cc, base + P + 64 * g:base + P + 64 * (g + 1)].rearrange("p (h d) -> p h d", d=4),
                            src[:, :, 8 + 4 * g:12 + 4 * g], ACT.Copy, scale=scale)
                    i.then_inc(s_for, 1)

        @block.tensor
        def _(pe):
            pe.wait_ge(s_const, 6)
            pe.wait_ge(s_asum, 2)
            pe.matmul(sm[:, 0:2], lhsT=ones[:, :], rhs=asum[:, :], start=True, stop=True).then_inc(s_sum, 1)
            for m in range(3):
                pe.wait_ge(s_down[m], 16)
                for k in range(4):
                    if 4 * m + k >= 2:
                        pe.wait_ge(s_tpr, 4 * m + k - 1)
                    for a in range(2):
                        for cc in range(CC):
                            i = pe.transpose(tp[k % 2][:, a * C + cc * P:a * C + (cc + 1) * P],
                                             down[m][:, cc, (2 * k + a) * P:(2 * k + a + 1) * P], w["ident"][:, :])
                    i.then_inc(s_tp, 1)
                pe.wait_ge(s_tpr, 4 * m + 4)
                if m == 0:
                    pe.wait_ge(s_upd, 18)
                n = 48 if m < 2 else 32
                for cc in range(CC):
                    if m:
                        pe.wait_ge(s_for, 2 * (m - 1) + cc + 1)
                    for hp in range(H // 2):
                        i = pe.matmul(fo[cc][:, hp * n:(hp + 1) * n], lhsT=downT[:, hp, cc * P:(cc + 1) * P],
                                      rhs=upd[m][:, :, :].rearrange("p a n -> p (a n)"), start=True, stop=True)
                    i.then_inc(s_fo, 1)
            pe.wait_ge(s_ter, 2)
            for cc in range(CC):
                for hc in range(HC):
                    i = pe.transpose(th[cc][:, hc * P:(hc + 1) * P], fter[:, hc, cc * P:(cc + 1) * P], idh[:, :])
                i.then_inc(s_th, 1)
            pv = pter[:, :, :].rearrange("p a (q k) -> p a k q", k=HC)
            for n in range(2):
                pe.wait_ge(s_thr, n + 1)
                for k in range(4):
                    for oc in range(2):
                        i = pe.transpose(th[n][:, k * C + oc * P:k * C + (oc + 1) * P], pv[:, oc, 4 * n + k, :], idh[:, :])
                i.then_inc(s_th, 1)
            pe.wait_ge(s_thr, 4)
            for hc in range(HC):
                pe.matmul(sm[:, 0:C], lhsT=ones[:, :], rhs=w["WP"][:, hc, 0:C], start=hc == 0, stop=hc == HC - 1)
            for hc in range(HC):
                i = pe.matmul(sm[:, C:2 * C], lhsT=ones[:, :], rhs=wb[:, hc, :], start=hc == 0, stop=hc == HC - 1)
            i.then_inc(s_cs, 1)


def project_and_feed_forward(nc, io, w, scr):
    with ExitStack() as ctx:
        def sb(name, shape, dt=fp32):
            return ctx.enter_context(nc.sbuf_tensor(name, shape, dt))

        def sem(name):
            return ctx.enter_context(nc.semaphore(name))

        X = [sb(f"x{i}", [P, SUB, C]) for i in range(2)]
        xn = sb("xn", [P, SUB, C])
        xT = sb("xT", [P, CC, CH])
        xh = sb("xh", [P, CC, CH], fp16)
        xl = sb("xl", [P, CC, CH], fp16)
        st6 = sb("st6", [P, SUB, 6])
        mv = sb("mv", [P, SUB, 2])
        ve = sb("ve", [P, SUB])
        rstd = sb("rstd", [P, SUB])
        nmr = sb("nmr", [P, SUB])
        part = [sb(f"part{i}", [P, PARTS, CH], bf16) for i in range(4)]
        rope = sb("rope", [P, CH])
        rot = sb("rot", [P, CH])
        rest = sb("rest", [P, CH])
        Vs = sb("Vs", [P, SUB, C])
        g = sb("g", [P, HC, CH])
        g2 = sb("g2", [P, HC, CH])
        fst = sb("fst", [P, SUB, 2])
        fmm = sb("fmm", [P, SUB])
        fve = sb("fve", [P, SUB])
        frs = sb("frs", [P, SUB])
        ft = sb("ft", [P, SUB, C])
        xc = sb("xc", [P, SUB, C])
        R = sb("R", [P, SUB, C])
        bank = [ctx.enter_context(nc.psum_tensor(f"bank{i}", [P, CH], fp32)) for i in range(8)]

        x_loaded = [sem(f"x_loaded{i}") for i in range(2)]
        stats_ready = sem("stats_ready")
        rstd_ready = sem("rstd_ready")
        fvar_ready = sem("fvar_ready")
        frs_ready = sem("frs_ready")
        xn_ready = sem("xn_ready")
        xT_in_psum = sem("xT_in_psum")
        xT_ready = sem("xT_ready")
        xhl_ready = sem("xhl_ready")
        qk_ready = sem("qk_ready")
        qk_read = sem("qk_read")
        part_ready = sem("part_ready")
        part_stored = sem("part_stored")
        v_ready = sem("v_ready")
        v_read = sem("v_read")
        v_stored = sem("v_stored")
        h_ready = sem("h_ready")
        h_read = sem("h_read")
        g2_ready = sem("g2_ready")
        ffn_ready = sem("ffn_ready")
        ffn_read = sem("ffn_read")
        R_ready = sem("R_ready")
        R_stored = sem("R_stored")
        steps = sem("dve_steps")
        block = ctx.enter_context(nc.Block())

        x_v = io["x"].rearrange("(n s p) c -> n p s c", p=P, s=SUB)
        R_v = scr["R"].rearrange("(n s p) c -> n p s c", p=P, s=SUB)
        V_v = scr["V"].rearrange("n (t s p) c -> n t p s c", p=P, s=SUB)
        qk_v = [scr[m].rearrange("a b (h e) t -> a b h e t", e=DH) for m in ("Q", "K")]
        STORES = 2 * 3 * PARTS

        @block.sync
        def _(sp):
            grant(sp, (R_ready, 1), (R_stored, 16), (v_stored, 16), (part_stored, 16))
            sp.dma_start(X[0][:, :, :], x_v[0]).then_inc(x_loaded[0], 16)
            with sp.Fori(0, NCH // 2) as i2:
                for par in range(2):
                    ch = i2 * 2 + par
                    sp.wait_ge(R_ready, ch + 1)
                    nxt = (ch + 1) % NCH
                    sp.dma_start(X[1 - par][:, None, :, :], x_v[bass.ds(nxt, 1), :, :, :].rearrange("n p s c -> p n s c"))\
                        .then_inc(x_loaded[1 - par], 16)
                    b, t = ch // TC, ch % TC
                    sp.wait_ge(v_read, ch * 2 + 2)
                    for hq in range(QB):
                        sp.dma_start(V_v[bass.ds(b * QB + hq, 1), bass.ds(t, 1), :, :, :].rearrange("n t p s c -> p (n t) s c"),
                                     Vs[:, None, :, hq * G * DH:(hq + 1) * G * DH]).then_inc(v_stored, 16)
                    for m in range(2):
                        for tile in range(2):
                            sp.wait_ge(part_ready, ch * 4 + 2 * m + tile + 1)
                            rows = [(0, P, 0, 8)] if tile == 0 else [(0, 64, 8, 4), (64, 64, 12, 4)]
                            for a in range(PARTS):
                                for p0, n, e0, ne in rows:
                                    dst = qk_v[m][a, bass.ds(b, 1), :, e0:e0 + ne, bass.ds(t * CH, CH)]
                                    sp.dma_start(dst, part[2 * m + tile][p0:p0 + n, a, :]).then_inc(part_stored, 16)
                    sp.wait_ge(R_ready, ch + 2)
                    sp.dma_start(R_v[bass.ds(ch, 1), :, :, :].rearrange("n p s c -> p n s c"), R[:, None, :, :])\
                        .then_inc(R_stored, 16)
            sp.wait_ge(x_loaded[0], 16 * (NCH // 2 + 1))
            sp.wait_ge(v_stored, 16 + 16 * QB * NCH)
            sp.wait_ge(part_stored, 16 + 16 * STORES * NCH)
            sp.wait_ge(R_stored, 16 + 16 * NCH)

        @block.gpsimd
        def _(pool):
            def rsqrt(out, in_):
                return pool.tensor_tensor(out=out[:, :], in0=in_[:, :], in1=w["mhalf"][:, :], op=ALU.pow)

            pool.wait_ge(stats_ready, 1)
            rsqrt(rstd, ve).then_inc(rstd_ready, 1)
            with pool.Fori(0, NCH) as ch:
                pool.wait_ge(stats_ready, ch + 2)
                rsqrt(rstd, ve).then_inc(rstd_ready, 1)
                pool.wait_ge(fvar_ready, ch + 1)
                rsqrt(frs, fve).then_inc(frs_ready, 1)

        @block.vector
        def _(dve):
            me = Steps(dve, steps, 22)
            spare = dve.alloc_register("spare_of_dve")

            def stats(x, chunk, loaded, count):
                dve.wait_ge(loaded, count)
                for s in range(SUB):
                    i = dve.bn_stats(st6[:, s, :], x[:, s, :])
                me.done(i)
                wait_apart(dve, spare, steps, me.base + me.n, x_loaded[0], 16)
                for s in range(SUB):
                    i = dve.bn_aggr(mv[:, s, :], st6[:, s, :])
                me.done(i)
                me.wait()
                dve.tensor_scalar(ve[:, :], mv[:, :, 1], LN_EPS, None, ALU.add).then_inc(stats_ready, 1)

            def normalise(x, count):
                dve.wait_ge(rstd_ready, count)
                me.done(dve.scalar_tensor_tensor(out=nmr[:, :], in0=mv[:, :, 0], scalar=-1.0, in1=rstd[:, :],
                                                 op0=ALU.mult, op1=ALU.mult))
                me.wait()
                for s in range(SUB):
                    i = dve.tensor_scalar(xn[:, s, :], x[:, s, :], rstd[:, s:s + 1], nmr[:, s:s + 1],
                                          ALU.mult, ALU.add)
                i.then_inc(xn_ready, 1)

            def split(src, dst):
                me.done(dve.tensor_copy(dst[:, 0, :], src))
                me.wait()
                last_read = dve.tensor_tensor(out=rest[:, :], in0=src, in1=dst[:, 0, :], op=ALU.subtract)
                return last_read

            def split_rest(dst):
                me.done(dve.tensor_copy(dst[:, 1, :], rest[:, :]))
                me.wait()
                return dve.tensor_tensor(out=dst[:, 2, :], in0=rest[:, :], in1=dst[:, 1, :], op=ALU.subtract)

            def tiles(m, ch, t):
                a, b, r = bank[3 * m % 4], bank[(3 * m + 1) % 4], bank[(3 * m + 2) % 4]
                dve.wait_ge(part_stored, ch * (16 * STORES) + 16)
                dve.wait_ge(qk_ready, ch * 6 + 3 * m + 1)
                split(a[:, :], part[2 * m]).then_inc(qk_read, 1)
                dve.wait_ge(qk_read, ch * 6 + 3 * m + 1)
                split_rest(part[2 * m]).then_inc(part_ready, 1)
                dve.wait_ge(qk_ready, ch * 6 + 3 * m + 2)
                dve.tensor_tensor(out=rope[:, :], in0=b[:, :], in1=w["cos"][:, t], op=ALU.mult).then_inc(qk_read, 1)
                dve.wait_ge(qk_ready, ch * 6 + 3 * m + 3)
                dve.tensor_tensor(out=rot[:, :], in0=r[:, :], in1=w["sin"][:, t], op=ALU.mult).then_inc(qk_read, 1)
                dve.wait_ge(qk_read, ch * 6 + 3 * m + 3)
                me.done(dve.tensor_tensor(out=rope[:, :], in0=rope[:, :], in1=rot[:, :], op=ALU.add))
                me.wait()
                me.done(split(rope[:, :], part[2 * m + 1]))
                me.wait()
                split_rest(part[2 * m + 1]).then_inc(part_ready, 1)

            dve.memset(xn[:, 0, 0:1], 0.0).then_inc(ffn_read, 4)
            stats(X[0], 0, x_loaded[0], 16)
            normalise(X[0], 1)
            assert me.n == 3
            first = me.n
            with dve.Fori(0, NCH // 2) as i2:
                for par in range(2):
                    ch = i2 * 2 + par
                    me.start(ch)
                    me.base = me.base + first
                    tokens = bass.ds((ch % TC) * CH, CH)
                    dve.wait_ge(xT_ready, ch * 2 + 2)
                    me.done(dve.tensor_copy(xh[:, :, :], xT[:, :, :]))
                    me.wait()
                    dve.tensor_tensor(out=xl[:, :, :], in0=xT[:, :, :], in1=xh[:, :, :], op=ALU.subtract)\
                        .then_inc(xhl_ready, 1)
                    tiles(0, ch, tokens)
                    stats(X[1 - par], ch + 1, x_loaded[1 - par], i2 * 16 + 16 + 16 * par)
                    tiles(1, ch, tokens)
                    dve.wait_ge(xT_in_psum, ch * 2 + 2)
                    normalise(X[1 - par], ch + 2)
                    for s in range(SUB):
                        dve.wait_ge(ffn_ready, ch * 4 + s + 1)
                        me.done(dve.tensor_copy(fst[:, s, :], bank[s][:, C:C + 2]))
                        me.wait()
                        dve.scalar_tensor_tensor(out=ft[:, s, :], in0=w["NB"][:, :], scalar=fst[:, s, 0:1],
                                                 in1=bank[s][:, 0:C], op0=ALU.mult, op1=ALU.add).then_inc(ffn_read, 1)
                    me.done(dve.tensor_tensor(out=fmm[:, :], in0=fst[:, :, 0], in1=fst[:, :, 0], op=ALU.mult))
                    me.wait()
                    dve.scalar_tensor_tensor(out=fve[:, :], in0=fst[:, :, 1], scalar=LN_EPS, in1=fmm[:, :],
                                             op0=ALU.add, op1=ALU.subtract).then_inc(fvar_ready, 1)
                    me.done(dve.tensor_tensor(out=xc[:, :, :], in0=X[par][:, :, :],
                                              in1=w["CB"][:, None, :].to_broadcast([P, SUB, C]), op=ALU.add))
                    me.wait()
                    dve.wait_ge(ffn_read, ch * 4 + 8)
                    dve.wait_ge(frs_ready, ch + 1)
                    dve.wait_ge(R_stored, ch * 16 + 16)
                    for s in range(SUB):
                        i = dve.scalar_tensor_tensor(out=R[:, s, :], in0=ft[:, s, :], scalar=frs[:, s:s + 1],
                                                     in1=xc[:, s, :], op0=ALU.mult, op1=ALU.add)
                    i.then_inc(R_ready, 1)
                    me.end()

        @block.scalar
        def _(act):
            def xT_evac(turn):
                for cc in range(CC):
                    act.wait_ge(xT_in_psum, turn * 2 + cc + 1)
                    act.activation(xT[:, cc, :], bank[4 + cc][:, :], ACT.Copy).then_inc(xT_ready, 1)

            xT_evac(0)
            with act.Fori(0, NCH) as ch:
                act.wait_ge(v_stored, ch * (16 * QB) + 16)
                for k in range(2):
                    act.wait_ge(v_ready, ch * 2 + k + 1)
                    act.activation(Vs[:, 2 * k:2 * k + 2, :], bank[4 + k][:, :].rearrange("p (s c) -> p s c", s=2),
                                   ACT.Copy).then_inc(v_read, 1)
                for hc in range(HC + 1):
                    if hc < HC:
                        act.wait_ge(h_ready, ch * HC + hc + 1)
                        act.activation(g[:, hc, :], bank[6 + hc % 2][:, :], ACT.Gelu).then_inc(h_read, 1)
                    if hc:
                        act.wait_ge(h_read, ch * HC + hc + 2)
                        act.activation(g2[:, hc - 1, :], g[:, hc - 1, :], ACT.Square).then_inc(g2_ready, 1)
                xT_evac(ch + 1)

        @block.tensor
        def _(pe):
            def transposes(turn):
                pe.wait_ge(xn_ready, turn + 1)
                for cc in range(CC):
                    for s in range(SUB):
                        i = pe.transpose(bank[4 + cc][:, s * P:(s + 1) * P], xn[:, s, cc * P:(cc + 1) * P], w["ident"][:, :])
                    i.then_inc(xT_in_psum, 1)

            pe.matmul(bank[6][:, 0:1], lhsT=w["ident"][:, :], rhs=w["ident"][:, 0:1], start=True, stop=True)\
                .then_inc(h_read, 2)
            transposes(0)
            with pe.Fori(0, NCH) as ch:
                pe.wait_ge(xT_ready, ch * 2 + 2)
                for t in range(6):
                    if t < 4:
                        pe.wait_ge(ffn_read, ch * 4 + t + 1)
                    else:
                        pe.wait_ge(qk_read, ch * 6 + t - 3)
                    for cc in range(CC):
                        i = pe.matmul(bank[t % 4][:, :], lhsT=w["WQK"][:, cc, t * P:(t + 1) * P], rhs=xT[:, cc, :],
                                      start=cc == 0, stop=cc == CC - 1)
                    i.then_inc(qk_ready, 1)
                for k in range(2):
                    for a in range(2):
                        s = 2 * k + a
                        for cc in range(CC):
                            i = pe.matmul(bank[4 + k][:, a * C:(a + 1) * C], lhsT=xT[:, cc, s * P:(s + 1) * P],
                                          rhs=w["WV"][:, cc, :], start=cc == 0, stop=cc == CC - 1)
                    i.then_inc(v_ready, 1)
                pe.wait_ge(xhl_ready, ch + 1)
                for hc in range(HC):
                    pe.wait_ge(h_read, ch * HC + hc + 1)
                    for k, (cc, x) in enumerate(((0, xh), (1, xh), (0, xl), (1, xl))):
                        i = pe.matmul(bank[6 + hc % 2][:, :], lhsT=w["WF"][:, cc, hc * P:(hc + 1) * P], rhs=x[:, cc, :],
                                      start=k == 0, stop=k == 3)
                    i.then_inc(h_ready, 1)
                pe.wait_ge(v_read, ch * 2 + 2)
                transposes(ch + 1)
                pe.wait_ge(g2_ready, ch * HC + HC)
                for s in range(SUB):
                    pe.wait_ge(qk_read, ch * 6 + (5, 6, 6, 6)[s])
                    for hc in range(HC):
                        pe.matmul(bank[s][:, 0:C + 1], lhsT=g[:, hc, s * P:(s + 1) * P], rhs=w["WP"][:, hc, :],
                                  start=hc == 0, stop=hc == HC - 1)
                    for hc in range(HC):
                        i = pe.matmul(bank[s][:, C + 1:C + 2], lhsT=g2[:, hc, s * P:(s + 1) * P], rhs=w["mean_col"][:, :],
                                      start=hc == 0, stop=hc == HC - 1)
                    i.then_inc(ffn_ready, 1)


ST, SM, PT = 2, 3, 6
SLOTS = 3
UNITS = sum(2 * G * (c + 1) for c in range(TC))
PAIRS = UNITS // 2
DIAG = 2 * SUB * TC
BLOCKS = [(h, t, k) for h in range(G) for t in range(T // P) for k in range(t // SUB + 1)]
NB = len(BLOCKS)
QROWS = (0, 0, 0, 1, 1, 2)
KROWS = (0, 1, 2, 0, 1, 0)
KD = len(QROWS) * DH


LAG = 2
ORDER = [(c, j, CH - P * max(0, j - SUB * c)) for c in range(TC) for j in range(SUB * (c + 1))]


def block_width(g):
    h, t, k = BLOCKS[g]
    return P * (t % SUB + 1) if k == t // SUB else CH


def plan_blocks():
    steps = []
    for n in range(PAIRS + LAG):
        if n < PAIRS:
            steps += [2 * ORDER[n][2]] * 2
        if n >= LAG:
            steps += [4 * ORDER[n - LAG][2]]
    total = sum(steps)
    work = [block_width(g) + 64 for g in range(NB)]
    plan, done, seen, g = [], 0, 0, 0
    for columns in steps:
        seen += columns
        share = min(1.0, seen / (SPREAD * total)) * sum(work)
        now = []
        while g < NB and done + work[g] / 2 <= share:
            now.append(g)
            done += work[g]
            g += 1
        plan.append(now)
    assert g == NB
    return plan


SPREAD = 0.93
PLAN = plan_blocks()


def attention(nc, w, scr):
    with ExitStack() as ctx:
        def sb(name, shape, dt=fp32):
            return ctx.enter_context(nc.sbuf_tensor(name, shape, dt))

        def sem(name):
            return ctx.enter_context(nc.semaphore(name))

        Q = [sb(f"Q{i}", [KD + 2, G, T], bf16) for i in range(SLOTS)]
        K = [sb(f"K{i}", [KD + 2, G, T], bf16) for i in range(SLOTS)]
        Vr = sb("V_raw", [P, T // P, G * DH])
        V = [sb(f"V{i}", [P, T // P, G, 2 * DH]) for i in range(SLOTS)]
        prob = [sb(f"prob{i}", [P, 2, CH]) for i in range(PT)]
        Y = sb("Y", [P, T])
        pm = sb("pm", [P, G, T // P, TC])
        m = sb("m", [P, P])
        mh = sb("mh", [G * T // P, P], bf16)
        ml = sb("ml", [G * T // P, P], bf16)
        idb = sb("idb", [P, P], bf16)
        mask = sb("mask", [P, P], bf16)
        st = [ctx.enter_context(nc.psum_tensor(f"st{i}", [P, 2, CH], fp32)) for i in range(ST)]
        sm = [ctx.enter_context(nc.psum_tensor(f"sm{i}", [P, CH], fp32)) for i in range(SM)]
        pv = ctx.enter_context(nc.psum_tensor("pv", [P, CH], fp32))

        consts = sem("consts")
        pool_steps = sem("pool_steps")
        qk_loaded = [sem(f"qk_loaded{i}") for i in range(SLOTS)]
        v_loaded = sem("v_loaded")
        v_placed = sem("v_placed")
        st_ready = sem("st_ready")
        exp_done = sem("exp_done")
        masked = sem("masked")
        pair_used = sem("pair_used")
        pv_read = sem("pv_read")
        y_stored = sem("y_stored")
        sm_ready = sem("sm_ready")
        sm_read = sem("sm_read")
        m_ready = sem("m_ready")
        mrow_hi = sem("mrow_hi")
        m_loaded = sem("m_loaded")
        block = ctx.enter_context(nc.Block())

        LOADS = 2 * len(QROWS)
        YS = 2 * G
        order = ORDER
        diag = [j >= SUB * c for c, j, _ in order]

        def quads(eng, body):
            with eng.Fori(0, NQ // SLOTS) as it:
                for k in range(SLOTS):
                    body(it * SLOTS + k, k, False)
            body(NQ - 1, (NQ - 1) % SLOTS, True)

        @block.sync
        def _(sp):
            def load_qk(quad, slot):
                b, hq = quad // QB, quad % QB
                for name, dst, rows in (("Q", Q, QROWS), ("K", K, KROWS)):
                    for r, a in enumerate(rows):
                        src = scr[name].rearrange("a b (q h e) t -> a b q e h t", h=G, e=DH)[a]
                        if isinstance(quad, int):
                            src = src[b, hq]
                        else:
                            src = src[bass.ds(b, 1), bass.ds(hq, 1), :, :, :].rearrange("b q e h t -> (b q e) h t")
                        sp.dma_start(dst[slot][r * DH:(r + 1) * DH, :, :], src).then_inc(qk_loaded[slot], 16)

            def load_v(quad):
                src = scr["V"].rearrange("n (j p) d -> n p j d", p=P)
                src = src[quad] if isinstance(quad, int) else \
                    src[bass.ds(quad, 1), :, :, :].rearrange("n p j d -> (n p) j d")
                sp.dma_start(Vr[:, :, :], src).then_inc(v_loaded, 16)

            def load_m(slot, count):
                sp.wait_ge(sm_read, count * (NB + 1) + SM)
                for r, src in enumerate((mh, ml)):
                    sp.dma_start(Q[slot][KD + r:KD + r + 1, :, :],
                                 src[:, :]).then_inc(m_loaded, 16)

            def body(quad, slot, last):
                if not last:
                    sp.wait_ge(pair_used, quad * PAIRS + PT // 2)
                    load_qk((quad + 2) % NQ, (slot + 2) % SLOTS)
                    sp.wait_ge(v_placed, quad + 1)
                    load_v(quad + 1)
                    load_m((slot + 1) % SLOTS, quad + 2)
                sp.wait_ge(pv_read, quad * TC + TC + 1)
                for h in range(G):
                    row = quad * (G * DH) + h * DH
                    sp.dma_start(scr["Y"][bass.ds(row, DH), :], Y[2 * DH * h:2 * DH * h + DH, :]).then_inc(y_stored, 16)
                    sp.dma_start(scr["L"][bass.ds(quad * G + h, 1), :],
                                 Y[2 * DH * h + DH:2 * DH * h + DH + 1, :]).then_inc(y_stored, 16)

            grant(sp, (pv_read, 1), (y_stored, 16))
            load_qk(0, 0)
            load_v(0)
            load_qk(1, 1)
            load_m(0, 1)
            quads(sp, body)
            sp.wait_ge(y_stored, 16 + 16 * YS * NQ)
            for s in range(SLOTS):
                sp.wait_ge(qk_loaded[s], 16 * LOADS * len([n for n in range(NQ + 1) if n % SLOTS == s]))

        @block.gpsimd
        def _(pool):
            spare = pool.alloc_register("spare_of_pool")
            for s in range(SLOTS):
                pool.memset(V[s][:, :, :, DH:2 * DH], 1.0)
            pool.memset(idb[:, :], 0.0).then_inc(pool_steps, 1)
            pool.memset(mask[:, :], 0.0).then_inc(pool_steps, 1)
            pool.wait_ge(pool_steps, 2)
            pool.affine_select(out=idb[:, :], in_=idb[:, :], compare_op=ALU.not_equal, fill=1.0, base=0,
                               pattern=[[-1, P]], channel_multiplier=1)
            pool.affine_select(out=mask[:, :], in_=mask[:, :], compare_op=ALU.is_ge, fill=-1e30, base=0,
                               pattern=[[-1, P]], channel_multiplier=1).then_inc(consts, 1)

            def place_v(quad, slot):
                wait_apart(pool, spare, v_loaded, quad * 16 + 16, pool_steps, 2)
                pool.tensor_copy(V[slot][:, :, :, 0:DH], Vr[:, :, :].rearrange("p j (h d) -> p j h d", h=G))\
                    .then_inc(v_placed, 1)

            def body(quad, slot, last):
                d = 0
                for n, (c, j, width) in enumerate(order):
                    if n == 4 and not last:
                        place_v(quad + 1, (slot + 1) % SLOTS)
                    if not diag[n]:
                        continue
                    for u in (2 * n, 2 * n + 1):
                        x = prob[(slot * UNITS + u) % PT][:, :, 0:P]
                        wait_apart(pool, spare, exp_done, quad * UNITS + (u + 1 + ST), pool_steps, 2)
                        pool.affine_select(out=x, in_=x, compare_op=ALU.is_ge, fill=0.0, base=0,
                                           pattern=[[0, 2], [1, P]], channel_multiplier=-1).then_inc(masked, 1)
                        d += 1
                assert d == DIAG

            place_v(0, 0)
            quads(pool, body)

        @block.scalar
        def _(act):
            def body(quad, slot, last):
                def evac(c):
                    ends = sum(x[0] <= c for x in order)
                    act.wait_ge(pair_used, quad * PAIRS + ends + PT // 2)
                    if c == 0:
                        act.wait_ge(y_stored, quad * (16 * YS) + 16)
                    act.activation(Y[:, c * CH:(c + 1) * CH], pv[:, :], ACT.Copy).then_inc(pv_read, 1)

                for n, (c, j, width) in enumerate(order):
                    act.wait_ge(pair_used, quad * PAIRS + n + 1)
                    for u in (2 * n, 2 * n + 1):
                        act.wait_ge(st_ready, quad * UNITS + u + 1)
                        act.activation(prob[(slot * UNITS + u) % PT][:, :, 0:width], st[u % ST][:, :, 0:width], ACT.Exp)\
                            .then_inc(exp_done, 1)
                    if n >= 2 and order[n - 2][0] != order[n - 1][0]:
                        evac(order[n - 2][0])
                evac(TC - 1)

            quads(act, body)

        @block.vector
        def _(dve):
            def block_max(g, base, ring):
                h, t, k = BLOCKS[g]
                width = P * (t % SUB + 1) if k == t // SUB else CH
                dve.wait_ge(sm_ready, base + g + 1)
                dve.tensor_reduce(out=pm[:, h, t, k:k + 1], in_=sm[(ring + g) % SM][:, 0:width], axis=AX.X, op=ALU.max)\
                    .then_inc(sm_read, 1)

            def row_max(quad, base, ring):
                dve.wait_ge(sm_read, base + NB + SM)
                dve.tensor_reduce(out=m[:, 0:G * T // P], in_=pm[:, :, :, :].rearrange("p h t k -> p (h t) k"), axis=AX.X, op=ALU.max)\
                    .then_inc(m_ready, 1)
                x = sm[(ring + NB) % SM][0:G * T // P, 0:P]
                dve.wait_ge(sm_ready, base + NB + 1)
                if not isinstance(quad, int):
                    dve.wait_ge(m_loaded, quad * 32)
                dve.tensor_scalar(mh[:, :], x, -1.0, None, ALU.mult).then_inc(mrow_hi, 1)
                dve.wait_ge(mrow_hi, quad + 1)
                dve.scalar_tensor_tensor(out=ml[:, :], in0=x, scalar=-1.0, in1=mh[:, :], op0=ALU.mult, op1=ALU.subtract)\
                    .then_inc(sm_read, 1)

            def maxima(quad, slot):
                base, ring = quad * (NB + 1), slot * (NB + 1)
                for g in range(NB):
                    block_max(g, base, ring)
                row_max(quad, base, ring)

            for s in range(SLOTS):
                dve.memset(K[s][KD:KD + 2, :, :], 1.0)
            dve.memset(m[:, :], 0.0)
            dve.memset(pm[:, :, :, :], -3e38).then_inc(sm_read, SM)
            maxima(0, 0)
            def body(quad, slot, last):
                if not last:
                    maxima(quad + 1, (slot + 1) % SLOTS)
            quads(dve, body)

        @block.tensor
        def _(pe):
            def scores_for_max(g, quad, slot):
                h, t, k = BLOCKS[g]
                last = k == t // SUB
                width = P * (t % SUB + 1) if last else CH
                dst = sm[(slot * (NB + 1) + g) % SM]
                pe.wait_ge(sm_read, quad * (NB + 1) + g + 1)
                i = pe.matmul(dst[:, 0:width], lhsT=Q[slot][0:KD, h, t * P:(t + 1) * P],
                              rhs=K[slot][0:KD, h, k * CH:k * CH + width], start=True, stop=not last)
                if last:
                    i = pe.matmul(dst[:, width - P:width], lhsT=idb[:, :], rhs=mask[:, :], start=False, stop=True)
                i.then_inc(sm_ready, 1)

            def transpose_m(quad, slot):
                pe.wait_ge(sm_read, quad * (NB + 1) + NB + 1)
                pe.wait_ge(m_ready, quad + 1)
                pe.transpose(sm[(slot * (NB + 1) + NB) % SM][:, 0:P], m[:, :], w["ident"][:, :])\
                    .then_inc(sm_ready, 1)

            def scores(quad, slot, u):
                c, j, width = order[u // 2]
                pe.wait_ge(exp_done, quad * UNITS + u + 1)
                for a in range(2):
                    h = 2 * (u % 2) + a
                    i = pe.matmul(st[u % ST][:, a, 0:width], lhsT=K[slot][:, h, j * P:(j + 1) * P],
                                  rhs=Q[slot][:, h, (c + 1) * CH - width:(c + 1) * CH], start=True, stop=True)
                i.then_inc(st_ready, 1)

            def weighted_sums(quad, slot, n):
                c, j, width = order[n]
                if j == 0:
                    pe.wait_ge(pv_read, quad * TC + c + 1)
                if diag[n]:
                    pe.wait_ge(masked, quad * DIAG + 2 * sum(diag[:n + 1]))
                else:
                    pe.wait_ge(exp_done, quad * UNITS + 2 * n + 2 + ST)
                for h in range(G):
                    i = pe.matmul(pv[2 * DH * h:2 * DH * (h + 1), CH - width:CH], lhsT=V[slot][:, j, h, :],
                                  rhs=prob[(slot * UNITS + 2 * n + h // 2) % PT][:, h % 2, 0:width],
                                  start=j == 0, stop=j == SUB * (c + 1) - 1, tile_position=(0, 2 * DH * h))
                    if h == G - 1:
                        i.then_inc(pair_used, 1)

            pe.wait_ge(consts, 1)
            pe.matmul(pv[:, 0:1], lhsT=idb[:, :], rhs=idb[:, 0:1], start=True, stop=True).then_inc(exp_done, ST)
            pe.matmul(pv[:, 0:1], lhsT=idb[:, :], rhs=idb[:, 0:1], start=True, stop=True).then_inc(pair_used, PT // 2)
            pe.wait_ge(qk_loaded[0], 16 * LOADS)
            for g in range(NB):
                scores_for_max(g, 0, 0)
            transpose_m(0, 0)

            def body(quad, slot, last):
                pe.wait_ge(m_loaded, quad * 32 + 32)
                pe.wait_ge(v_placed, quad + 1)
                if not last:
                    turn = quad // SLOTS
                    nxt = (slot + 1) % SLOTS
                    pe.wait_ge(qk_loaded[nxt], (turn + (2 if nxt == 0 else 1)) * (16 * LOADS))
                plan = iter(PLAN)

                def next_blocks():
                    for g in () if last else next(plan):
                        scores_for_max(g, quad + 1, nxt)

                for n in range(PAIRS + LAG):
                    for u in (2 * n, 2 * n + 1) if n < PAIRS else ():
                        scores(quad, slot, u)
                        next_blocks()
                    if not last and n == PAIRS - 1:
                        transpose_m(quad + 1, nxt)
                    if n >= LAG:
                        weighted_sums(quad, slot, n - LAG)
                        next_blocks()

            quads(pe, body)


def project_out(nc, io, w, scr):
    with ExitStack() as ctx:
        def sb(name, shape, dt=fp32):
            return ctx.enter_context(nc.sbuf_tensor(name, shape, dt))

        def sem(name):
            return ctx.enter_context(nc.semaphore(name))

        Wc = sb("Wc", [P, CC, C])
        Lall = sb("Lall", [P, NQ * G * T // P])
        Rall = sb("Rall", [P, NQ * G * T // P])
        ones = sb("ones16", [H, CC, H // CC, DH])
        E = sb("E", [H, CC, H // CC, DH])
        Y = [sb(f"Yt{i}", [P, CC, CH]) for i in range(2)]
        rl = [sb(f"rl{i}", [H, CH]) for i in range(2)]
        Yn = [sb(f"Yn{i}", [P, CC, CH]) for i in range(2)]
        R = [sb(f"Rt{i}", [P, SUB, C]) for i in range(2)]
        out = [sb(f"out{i}", [P, SUB, C]) for i in range(2)]
        pr = [ctx.enter_context(nc.psum_tensor(f"pr{i}", [P, CH], fp32)) for i in range(4)]
        po = [ctx.enter_context(nc.psum_tensor(f"po{i}", [P, 2, C], fp32)) for i in range(4)]
        wc_loaded = sem("wc_loaded")
        l_loaded = sem("l_loaded")
        l_inverted = sem("l_inverted")
        l_stored = sem("l_stored")
        e_ready = sem("e_ready")
        in_loaded = [sem(f"in_loaded{i}") for i in range(2)]
        spread = sem("spread")
        normed = sem("normed")
        projected = sem("projected")
        added = sem("added")
        out_stored = [sem(f"out_stored{i}") for i in range(2)]
        block = ctx.enter_context(nc.Block())
        R_v = scr["R"].rearrange("(n s p) c -> n p s c", p=P, s=SUB)
        O_v = io["out"].rearrange("(n s p) c -> n p s c", p=P, s=SUB)
        Y_v = scr["Y"].rearrange("(b a p) (t q) -> b t p a q", p=P, a=CC, q=CH)
        L_v = scr["RL"].rearrange("(b h) (t q) -> b t h q", h=H, q=CH)
        L_flat = [scr[n].rearrange("h (a t) -> (h a) t", a=P // (B * H)) for n in ("L", "RL")]

        @block.sync
        def _(sp):
            grant(sp, (added, 3), (out_stored[0], 16), (out_stored[1], 16))
            sp.dma_start(Lall[:, :], L_flat[0]).then_inc(l_loaded, 16)
            sp.dma_start(Wc[:, :, :], io["Wc"].rearrange("(a p) c -> p a c", p=P)).then_inc(wc_loaded, 16)
            sp.wait_ge(l_inverted, 1)
            sp.dma_start(L_flat[1], Rall[:, :]).then_inc(l_stored, 16)
            sp.wait_ge(l_stored, 16)
            with sp.Fori(0, NCH // 2) as i2:
                for par in range(2):
                    ch = i2 * 2 + par
                    b, t = ch // TC, ch % TC
                    sp.wait_ge(added, ch * 2 + 1)
                    sp.dma_start(Y[par][:, None, :, :], Y_v[bass.ds(b, 1), bass.ds(t, 1), :, :, :].rearrange("b t p a q -> p (b t) a q"))\
                        .then_inc(in_loaded[par], 16)
                    sp.dma_start(rl[par][:, None, :], L_v[bass.ds(b, 1), bass.ds(t, 1), :, :].rearrange("b t h q -> h (b t) q"))\
                        .then_inc(in_loaded[par], 16)
                    sp.dma_start(R[par][:, None, :, :], R_v[bass.ds(ch, 1), :, :, :].rearrange("n p s c -> p n s c"))\
                        .then_inc(in_loaded[par], 16)

        @block.gpsimd
        def _(pool):
            pool.memset(ones[:, :, :, :], 1.0).then_inc(e_ready, 1)
            pool.wait_ge(e_ready, 1)
            pool.affine_select(out=E[:, :, :, :], in_=ones[:, :, :, :], compare_op=ALU.is_equal, fill=0.0, base=0,
                               pattern=[[-(H // CC), CC], [-1, H // CC], [0, DH]], channel_multiplier=1).then_inc(e_ready, 1)

        @block.vector
        def _(dve):
            dve.wait_ge(l_loaded, 16)
            dve.reciprocal(Rall[:, :], Lall[:, :]).then_inc(l_inverted, 1)
            with dve.Fori(0, NCH // 2) as i2:
                for par in range(2):
                    ch = i2 * 2 + par
                    dve.wait_ge(in_loaded[par], i2 * 48 + 48)
                    for a in range(CC):
                        dve.wait_ge(spread, ch * 2 + a + 1)
                        dve.tensor_tensor(out=Yn[par][:, a, :], in0=Y[par][:, a, :], in1=pr[2 * par + a][:, :], op=ALU.mult)\
                            .then_inc(normed, 1)
                    dve.wait_ge(out_stored[par], i2 * 16 + 16)
                    for k in range(2):
                        dve.wait_ge(projected, ch * 2 + k + 1)
                        dve.tensor_tensor(out=out[par][:, 2 * k:2 * k + 2, :], in0=R[par][:, 2 * k:2 * k + 2, :],
                                          in1=po[2 * par + k][:, :, :], op=ALU.add).then_inc(added, 1)

        @block.scalar
        def _(act):
            with act.Fori(0, NCH // 2) as i2:
                for par in range(2):
                    ch = i2 * 2 + par
                    act.wait_ge(added, ch * 2 + 5)
                    act.dma_start(O_v[bass.ds(ch, 1), :, :, :].rearrange("n p s c -> p n s c"), out[par][:, None, :, :])\
                        .then_inc(out_stored[par], 16)
            for par in range(2):
                act.wait_ge(out_stored[par], 16 + 16 * (NCH // 2))

        @block.tensor
        def _(pe):
            pe.wait_ge(e_ready, 2)
            pe.wait_ge(wc_loaded, 16)
            with pe.Fori(0, NCH // 2) as i2:
                for par in range(2):
                    ch = i2 * 2 + par
                    pe.wait_ge(in_loaded[par], i2 * 48 + 48)
                    for a in range(CC):
                        pe.matmul(pr[2 * par + a][:, :], lhsT=E[:, a, :, :].rearrange("k h d -> k (h d)"), rhs=rl[par][:, :],
                                  start=True, stop=True).then_inc(spread, 1)
                    pe.wait_ge(normed, ch * 2 + 2)
                    for k in range(2):
                        for s in range(2):
                            for a in range(CC):
                                i = pe.matmul(po[2 * par + k][:, s, :], lhsT=Yn[par][:, a, (2 * k + s) * P:(2 * k + s + 1) * P],
                                              rhs=Wc[:, a, :], start=a == 0, stop=a == CC - 1)
                        i.then_inc(projected, 1)


def build(nc, io):
    scr = {
        "Q": nc.dram_tensor("scratch_q", (PARTS, B, H * DH, T), bf16).ap(),
        "K": nc.dram_tensor("scratch_k", (PARTS, B, H * DH, T), bf16).ap(),
        "V": nc.dram_tensor("scratch_v", (NQ, T, G * DH), fp32).ap(),
        "R": nc.dram_tensor("scratch_r", (B * T, C), fp32).ap(),
        "Y": nc.dram_tensor("scratch_y", (B * H * DH, T), fp32).ap(),
        "L": nc.dram_tensor("scratch_l", (B * H, T), fp32).ap(),
        "RL": nc.dram_tensor("scratch_rl", (B * H, T), fp32).ap(),
    }
    with ExitStack() as ctx:
        w = {"ident": ctx.enter_context(nc.sbuf_tensor("ident", [P, P], fp32))}
        with ExitStack() as early:
            for name, shape, dt in (("mhalf", [P, SUB], fp32), ("mean_col", [P, 1], fp32), ("WQK", [P, CC, 6 * P], fp32),
                                    ("WV", [P, CC, C], fp32), ("WF", [P, CC, HID], fp16), ("WP", [P, HC, C + 1], fp32),
                                    ("NB", [P, C], fp32), ("CB", [P, C], fp32), ("cos", [P, T], fp32), ("sin", [P, T], fp32)):
                w[name] = early.enter_context(nc.sbuf_tensor("w" + name, shape, dt))
            make_weights(nc, io, w)
            project_and_feed_forward(nc, io, w, scr)
        attention(nc, w, scr)
        project_out(nc, io, w, scr)


_INS = {"x": "L0_attn_x", "Wq_down": "L0_attn_Wq_down", "Wk_down": "L0_attn_Wk_down", "Wv_down": "L0_attn_Wv_down",
        "Wq_up_c": "L0_attn_Wq_up_c", "Wq_up_e": "L0_attn_Wq_up_e", "Wk_up_c": "L0_attn_Wk_up_c",
        "Wk_up_e": "L0_attn_Wk_up_e", "Wv_up": "L0_attn_Wv_up", "Wc": "L0_attn_Wc", "W_fc": "L0_ffn_W_fc",
        "ln_w": "L0_ffn_ln_w", "ln_b": "L0_ffn_ln_b", "W_proj": "L0_ffn_W_proj"}


def _rope_tables():
    import numpy as np
    half = DH // 2
    inv = (1.0 / np.float32(10000.0) ** (np.arange(0, half, 2, dtype=np.float32) / np.float32(half))).astype(np.float32)
    emb = np.concatenate([np.arange(T, dtype=np.float32)[:, None] * inv] * 2, axis=-1)
    dim = np.array([2 * (r % 4) + r // 64 for r in range(P)])
    return [np.ascontiguousarray(f(emb)[:, dim].T.astype(np.float32)) for f in (np.cos, np.sin)]


def kernel(**inputs):
    import numpy as _np
    import concourse.bacc as _bacc
    from concourse import mybir as _mybir
    from concourse.bass_utils import run_bass_kernel_spmd as _run

    nc = _bacc.Bacc("TRN2", target_bir_lowering=False, num_devices=1)
    arrays, io = {}, {}
    for short, name in _INS.items():
        arrays[f"in_{short}"] = _np.ascontiguousarray(inputs[name])
    shape = arrays["in_x"].shape
    arrays["in_x"] = arrays["in_x"].reshape(-1, shape[-1])
    arrays["in_cos"], arrays["in_sin"] = _rope_tables()
    for name, a in arrays.items():
        io[name[3:]] = nc.dram_tensor(name, a.shape, _mybir.dt.from_np(a.dtype), kind="ExternalInput").ap()
    io["out"] = nc.dram_tensor("out_0", arrays["in_x"].shape, _mybir.dt.float32, kind="ExternalOutput").ap()
    build(nc, io)
    r = _run(nc, [arrays], core_ids=[0])
    return r.results[0]["out_0"].reshape(shape)
```

```python
import concourse.bass as bass
from concourse import mybir
from contextlib import ExitStack

fp32 = mybir.dt.float32
fp16 = mybir.dt.float16
bf16 = mybir.dt.bfloat16
ALU = mybir.AluOpType
ACT = mybir.ActivationFunctionType
AX = mybir.AxisListType

P = 128
B, T, C = 4, 2048, 256
H, L, DH = 16, 64, 16
HID = 1024
CC = C // P
HC = HID // P
CH = 512
NCH = B * T // CH
SUB = CH // P
TC = T // CH
G = 4
NQ = B * H // G
QB = H // G
PARTS = 3
LN_EPS = 1e-5
W_EPS = 1e-6


def grant(eng, *credits):
    for sem, value in credits:
        eng.nop().then_inc(sem, value)


class Steps:

    def __init__(self, eng, sem, per):
        self.eng, self.sem, self.per, self.n, self.base = eng, sem, per, 0, 0

    def start(self, turn):
        self.base, self.n = turn * self.per, 0

    def done(self, instruction):
        self.n += 1
        instruction.then_inc(self.sem, 1)

    def wait(self):
        self.eng.wait_ge(self.sem, self.base + self.n)

    def end(self):
        assert self.n == self.per, (self.n, self.per)


def wait_apart(eng, spare, sem, count, past, value):
    if not isinstance(count, int):
        count = eng.snap(count)
    eng.reg_mov(spare, count)
    eng.wait_ge(past, value)
    eng.wait_ge(sem, count)


def make_weights(nc, io, w):
    with ExitStack() as ctx:
        def sb(name, shape, dt=fp32):
            return ctx.enter_context(nc.sbuf_tensor(name, shape, dt))

        def sem(name):
            return ctx.enter_context(nc.semaphore(name))

        down = [sb(f"w_down{m}", [P, CC, H * L]) for m in range(3)]
        downT = sb("w_downT", [P, H // 2, C])
        up = [sb(f"w_up{m}", [P, 16]) for m in range(3)]
        upd = [sb(f"w_upd{m}", [P, 2, DH]) for m in range(3)]
        fc = sb("w_fc_raw", [P, HC, C])
        pj = sb("w_proj_raw", [P, CC, HID])
        fneg = sb("w_fneg", [P, HC, C], fp16)
        fter = sb("w_fter", [P, HC, C], fp16)
        pneg = sb("w_pneg", [P, CC, HID], fp16)
        pter = sb("w_pter", [P, CC, HID], fp16)
        lnw = sb("w_lnw", [P, HC])
        lnb = sb("w_lnb", [P, HC])
        wb = sb("w_bias_rows", [P, HC, C])
        ww = sb("w_scale_rows", [P, HC, C])
        wrec = sb("w_wrec", [P, 1])
        wmax = sb("w_wmax", [P, 1])
        asum = sb("w_asum", [P, 2])
        thr = sb("w_thr", [P, 2])
        nthr = sb("w_nthr", [P, 2])
        ones = sb("w_ones", [P, P])
        idh = sb("w_idh", [P, P], fp16)
        tp = [ctx.enter_context(nc.psum_tensor(f"wp_t{i}", [P, CH], fp32)) for i in range(2)]
        fo = [ctx.enter_context(nc.psum_tensor(f"wp_f{i}", [P, CH], fp32)) for i in range(2)]
        th = [ctx.enter_context(nc.psum_tensor(f"wp_h{i}", [P, 1024], fp16)) for i in range(2)]
        sm = ctx.enter_context(nc.psum_tensor("wp_s", [P, CH], fp32))

        s_down = [sem(f"w_down_loaded{m}") for m in range(3)]
        s_up = sem("w_up_loaded")
        s_ff = sem("w_ff_loaded")
        s_misc = sem("w_misc_loaded")
        s_const = sem("w_const_ready")
        s_pool = sem("w_pool_steps")
        s_dve = sem("w_dve_steps")
        s_upd = sem("w_upd_ready")
        s_asum = sem("w_asum_ready")
        s_sum = sem("w_sum_ready")
        s_ter = sem("w_ternary_ready")
        s_tp = sem("w_transposed")
        s_tpr = sem("w_transposed_read")
        s_fo = sem("w_folded")
        s_for = sem("w_folded_read")
        s_th = sem("w_ternary_transposed")
        s_thr = sem("w_ternary_transposed_read")
        s_cs = sem("w_column_sums")
        s_wmax = sem("w_wmax_rows")
        s_wall = sem("w_wmax_all")
        block = ctx.enter_context(nc.Block())

        ups = [("Wq_up_c", "Wq_up_e"), ("Wk_up_c", "Wk_up_e"), ("Wv_up",)]

        @block.sync
        def _(sp):
            sp.dma_start(fc[:, :, :], io["W_fc"].rearrange("(p a) c -> p a c", a=HC)).then_inc(s_ff, 16)
            sp.dma_start(pj[:, :, :], io["W_proj"].rearrange("(a p) h -> p a h", p=P)).then_inc(s_ff, 16)
            for m, names in enumerate(ups):
                for half in range(2):
                    for k, name in enumerate(names):
                        wide = io[name].shape[1]
                        sp.dma_start(up[m][64 * half:64 * half + 64, k * wide:(k + 1) * wide],
                                     io[name]).then_inc(s_up, 16)
            for m, name in enumerate(("Wq_down", "Wk_down", "Wv_down")):
                sp.dma_start(down[m][:, :, :], io[name].rearrange("(a p) n -> p a n", p=P)).then_inc(s_down[m], 16)
            sp.dma_start(lnw[:, :], io["ln_w"].rearrange("(p a) -> p a", a=HC)).then_inc(s_misc, 16)
            sp.dma_start(lnb[:, :], io["ln_b"].rearrange("(p a) -> p a", a=HC)).then_inc(s_misc, 16)
            sp.dma_start(w["cos"][:, :], io["cos"]).then_inc(s_misc, 16)
            sp.dma_start(w["sin"][:, :], io["sin"]).then_inc(s_misc, 16)
            x_v = io["x"].rearrange("(n s p) c -> n p s c", p=P, s=SUB)
            for k in range(2):
                sp.dma_start(w["X"][k][:, :, :], x_v[k]).then_inc(w["x_loaded"][k], 16)
            sp.wait_ge(s_misc, 64)

        @block.gpsimd
        def _(pool):
            pool.memset(w["ident"][:, :], 0.0).then_inc(s_pool, 1)
            pool.memset(idh[:, :], 0.0).then_inc(s_pool, 1)
            pool.wait_ge(s_pool, 2)
            for m in (w["ident"], idh):
                pool.affine_select(out=m[:, :], in_=m[:, :], compare_op=ALU.not_equal, fill=1.0, base=0,
                                   pattern=[[-1, P]], channel_multiplier=1).then_inc(s_const, 1)
            pool.memset(ones[:, :], 1.0).then_inc(s_const, 1)
            pool.memset(w["mhalf"][:, :], -0.5).then_inc(s_const, 1)
            pool.memset(w["mean_col"][:, :], 1.0 / HID).then_inc(s_const, 1)
            pool.wait_ge(s_wmax, 1)
            pool.partition_all_reduce(w["wall"][:, :], wmax[:, :], P, bass.bass_isa.ReduceOp.max).then_inc(s_wall, 1)

        @block.vector
        def _(dve):
            me = Steps(dve, s_dve, 0)
            for m in range(3):
                me.done(dve.memset(upd[m][:, :, :], 0.0))
            dve.wait_ge(s_ff, 32)
            dve.tensor_reduce(out=asum[:, 0:1], in_=fc[:, :, :], axis=AX.XY, op=ALU.add,
                              apply_absolute_value=True).then_inc(s_asum, 1)
            dve.tensor_reduce(out=asum[:, 1:2], in_=pj[:, :, :], axis=AX.XY, op=ALU.add,
                              apply_absolute_value=True).then_inc(s_asum, 1)
            dve.wait_ge(s_up, 16 * 10)
            me.wait()
            for m in range(3):
                for half in range(2):
                    r = slice(64 * half, 64 * half + 64)
                    if m == 2:
                        dve.tensor_copy(upd[m][r, half, :], up[m][r, :]).then_inc(s_upd, 1)
                        continue
                    eo = up[m][r, 8:16].rearrange("p (d g) -> p g d", g=2)
                    dve.tensor_copy(upd[m][r, half, 0:8], up[m][r, 0:8]).then_inc(s_upd, 1)
                    dve.tensor_copy(upd[m][r, half, 8:16].rearrange("p (g d) -> p g d", g=2), eo).then_inc(s_upd, 1)
            dve.wait_ge(s_sum, 1)
            me.done(dve.tensor_scalar(thr[:, :], sm[:, 0:2], 0.5 / (HID * C), 0.5 * W_EPS, ALU.mult, ALU.add))
            me.wait()
            me.done(dve.tensor_scalar(nthr[:, :], thr[:, :], -1.0, None, ALU.mult))
            me.wait()
            for n, (raw, neg, ter) in enumerate(((fc, fneg, fter), (pj, pneg, pter))):
                flat = [t[:, :, :].rearrange("p a b -> p (a b)") for t in (raw, neg, ter)]
                me.done(dve.tensor_scalar(flat[1], flat[0], nthr[:, n:n + 1], None, ALU.is_lt))
                me.wait()
                dve.scalar_tensor_tensor(out=flat[2], in0=flat[0], scalar=thr[:, n:n + 1], in1=flat[1],
                                         op0=ALU.is_gt, op1=ALU.subtract).then_inc(s_ter, 1)
            dve.wait_ge(s_misc, 64)
            dve.tensor_reduce(out=wmax[:, :], in_=lnw[:, :], axis=AX.X, op=ALU.max, apply_absolute_value=True)\
                .then_inc(s_wmax, 1)
            dve.wait_ge(s_wall, 1)
            me.done(dve.tensor_scalar(w["wmax"][:, :], w["wall"][:, :], 1e-30, None, ALU.max))
            me.wait()
            me.done(dve.reciprocal(wrec[:, :], w["wmax"][:, :]))
            me.wait()
            me.done(dve.tensor_scalar(w["lnw"][:, :], lnw[:, :], wrec[:, 0:1], None, ALU.mult))
            me.wait()
            for n in range(2):
                dve.wait_ge(s_th, n + 1)
                dve.tensor_copy(w["WF"][:, n, :], th[n % 2][:, :]).then_inc(s_thr, 1)
            for n in range(2):
                dve.wait_ge(s_th, 3 + n)
                for k in range(4):
                    hc = 4 * n + k
                    src = th[n % 2][:, k * C:(k + 1) * C]
                    dve.tensor_copy(w["WP"][:, hc, :], src)
                    dve.tensor_scalar(ww[:, hc, :], src, w["lnw"][:, hc:hc + 1], None, ALU.mult)
                    i = dve.tensor_scalar(wb[:, hc, :], src, lnb[:, hc:hc + 1], None, ALU.mult)
                i.then_inc(s_thr, 1)
            dve.wait_ge(s_cs, 1)
            dve.tensor_scalar(w["NB"][:, :], sm[:, 0:C], -1.0, None, ALU.mult)
            dve.tensor_copy(w["CB"][:, :], sm[:, C:2 * C]).then_inc(s_cs, 1)

        @block.scalar
        def _(act):
            for m in range(3):
                for k in range(4):
                    act.wait_ge(s_tp, 4 * m + k + 1)
                    if m and k == 0:
                        act.wait_ge(s_fo, 2 * m)
                    act.activation(downT[:, 2 * k:2 * k + 2, :],
                                   tp[k % 2][:, :].rearrange("p (a c) -> p a c", a=2), ACT.Copy).then_inc(s_tpr, 1)
                for cc in range(CC):
                    act.wait_ge(s_fo, 2 * m + cc + 1)
                    if m == 2:
                        act.activation(w["WV"][:, cc, :], fo[cc][:, 0:C], ACT.Copy).then_inc(s_for, 1)
                        continue
                    scale = float(DH) ** -0.5 if m == 0 else 1.0
                    base = m * 2 * P
                    src = fo[cc][:, 0:H * DH].rearrange("p (h e) -> p h e", e=DH)
                    act.activation(w["WQK"][:, cc, base:base + P].rearrange("p (h e) -> p h e", e=8),
                                   src[:, :, 0:8], ACT.Copy, scale=scale)
                    for g in range(2):
                        i = act.activation(
                            w["WQK"][:, cc, base + P + 64 * g:base + P + 64 * (g + 1)].rearrange("p (h d) -> p h d", d=4),
                            src[:, :, 8 + 4 * g:12 + 4 * g], ACT.Copy, scale=scale)
                    i.then_inc(s_for, 1)

        @block.tensor
        def _(pe):
            pe.wait_ge(s_const, 5)
            pe.wait_ge(s_asum, 2)
            pe.matmul(sm[:, 0:2], lhsT=ones[:, :], rhs=asum[:, :], start=True, stop=True).then_inc(s_sum, 1)
            def fold(m):
                pe.wait_ge(s_down[m], 16)
                for k in range(4):
                    if 4 * m + k >= 2:
                        pe.wait_ge(s_tpr, 4 * m + k - 1)
                    for a in range(2):
                        for cc in range(CC):
                            i = pe.transpose(tp[k % 2][:, a * C + cc * P:a * C + (cc + 1) * P],
                                             down[m][:, cc, (2 * k + a) * P:(2 * k + a + 1) * P], w["ident"][:, :])
                    i.then_inc(s_tp, 1)
                pe.wait_ge(s_tpr, 4 * m + 4)
                if m == 0:
                    pe.wait_ge(s_upd, 10)
                n = 2 * DH
                for cc in range(CC):
                    if m:
                        pe.wait_ge(s_for, 2 * (m - 1) + cc + 1)
                    for hp in range(H // 2):
                        i = pe.matmul(fo[cc][:, hp * n:(hp + 1) * n], lhsT=downT[:, hp, cc * P:(cc + 1) * P],
                                      rhs=upd[m][:, :, :].rearrange("p a n -> p (a n)"), start=True, stop=True)
                    i.then_inc(s_fo, 1)

            def transpose_fc():
                pe.wait_ge(s_ter, 2)
                for cc in range(CC):
                    for hc in range(HC):
                        i = pe.transpose(th[cc][:, hc * P:(hc + 1) * P], fter[:, hc, cc * P:(cc + 1) * P], idh[:, :])
                    i.then_inc(s_th, 1)

            def transpose_proj():
                pv = pter[:, :, :].rearrange("p a (q k) -> p a k q", k=HC)
                for n in range(2):
                    pe.wait_ge(s_thr, n + 1)
                    for k in range(4):
                        for oc in range(2):
                            i = pe.transpose(th[n][:, k * C + oc * P:k * C + (oc + 1) * P], pv[:, oc, 4 * n + k, :], idh[:, :])
                    i.then_inc(s_th, 1)

            fold(0)
            transpose_fc()
            fold(1)
            transpose_proj()
            fold(2)
            pe.wait_ge(s_thr, 4)
            for hc in range(HC):
                pe.matmul(sm[:, 0:C], lhsT=ones[:, :], rhs=ww[:, hc, :], start=hc == 0, stop=hc == HC - 1)
            for hc in range(HC):
                i = pe.matmul(sm[:, C:2 * C], lhsT=ones[:, :], rhs=wb[:, hc, :], start=hc == 0, stop=hc == HC - 1)
            i.then_inc(s_cs, 1)


def project_and_feed_forward(nc, io, w, scr):
    with ExitStack() as ctx:
        def sb(name, shape, dt=fp32):
            return ctx.enter_context(nc.sbuf_tensor(name, shape, dt))

        def sem(name):
            return ctx.enter_context(nc.semaphore(name))

        X, x_loaded = w["X"], w["x_loaded"]
        xn = sb("xn", [P, SUB, C])
        xT = sb("xT", [P, CC, CH])
        xh = sb("xh", [P, CC, CH], fp16)
        xl = sb("xl", [P, CC, CH], fp16)
        st6 = sb("st6", [P, SUB, 6])
        mv = sb("mv", [P, SUB, 2])
        ve = sb("ve", [P, SUB])
        rstd = sb("rstd", [P, SUB])
        nmr = sb("nmr", [P, SUB])
        part = [sb(f"part{i}", [P, PARTS, CH], bf16) for i in range(4)]
        rope = sb("rope", [P, CH])
        rot = sb("rot", [P, CH])
        rest = sb("rest", [P, CH])
        plain_rest = sb("plain_rest", [P, CH])
        Vs = sb("Vs", [P, SUB, C])
        g = sb("g", [P, HC, 2, CH])
        gh = sb("gh", [P, HC, CH], fp16)
        gl = sb("gl", [P, HC, CH], fp16)
        gsum = sb("gsum", [P, 2, CH])
        fst = sb("fst", [P, SUB, 2])
        fmm = sb("fmm", [P, SUB])
        fve = sb("fve", [P, SUB])
        frs = sb("frs", [P, SUB])
        frw = sb("frw", [P, SUB])
        ft = sb("ft", [P, SUB, C])
        xc = [sb(f"xc{i}", [P, SUB, C]) for i in range(2)]
        R = sb("R", [P, SUB, C])
        bank = [ctx.enter_context(nc.psum_tensor(f"bank{i}", [P, CH], fp32)) for i in range(8)]

        stats_ready = sem("stats_ready")
        rstd_ready = sem("rstd_ready")
        fvar_ready = sem("fvar_ready")
        frs_ready = sem("frs_ready")
        xn_ready = sem("xn_ready")
        xT_in_psum = sem("xT_in_psum")
        xT_ready = sem("xT_ready")
        xl_ready = sem("xl_ready")
        qk_ready = sem("qk_ready")
        high_ready = sem("high_ready")
        qk_read = sem("qk_read")
        part_ready = sem("part_ready")
        part_stored = sem("part_stored")
        v_ready = sem("v_ready")
        v_read = sem("v_read")
        v_stored = sem("v_stored")
        h_ready = sem("h_ready")
        h_read = sem("h_read")
        gh_ready = sem("gh_ready")
        g2_ready = sem("g2_ready")
        gl_ready = sem("gl_ready")
        gsum_ready = sem("gsum_ready")
        xc_ready = sem("xc_ready")
        ffn_ready = sem("ffn_ready")
        ffn_read = sem("ffn_read")
        R_ready = sem("R_ready")
        R_stored = sem("R_stored")
        steps = sem("dve_steps")
        pool_steps = sem("pool_steps_p")
        hidden_bank = [bank[i] for i in (6, 7, 4, 5)]
        block = ctx.enter_context(nc.Block())

        x_v = io["x"].rearrange("(n s p) c -> n p s c", p=P, s=SUB)
        R_v = scr["R"].rearrange("(n s p) c -> n p s c", p=P, s=SUB)
        V_v = scr["V"].rearrange("n (t s p) c -> n t p s c", p=P, s=SUB)
        qk_v = [scr[m].rearrange("a b (h e) t -> a b h e t", e=DH) for m in ("Q", "K")]
        STORES = 2 * 3 * PARTS

        @block.sync
        def _(sp):
            grant(sp, (R_ready, 1), (R_stored, 16), (v_stored, 16), (part_stored, 16))
            def body(ch, par):
                sp.wait_ge(xn_ready, ch + 1)
                sp.wait_ge(xc_ready, ch + 1)
                sp.dma_start(X[par][:, None, :, :], x_v[bass.ds((ch + 2) % NCH, 1), :, :, :].rearrange("n p s c -> p n s c"))\
                    .then_inc(x_loaded[par], 16)
                b, t = ch // TC, ch % TC

                def store_part(m, tile):
                    sp.wait_ge(part_ready, ch * 4 + 2 * m + tile + 1)
                    rows = [(0, P, 0, 8)] if tile == 0 else [(0, 64, 8, 4), (64, 64, 12, 4)]
                    for a in range(PARTS):
                        for p0, n, e0, ne in rows:
                            dst = qk_v[m][a, bass.ds(b, 1), :, e0:e0 + ne, bass.ds(t * CH, CH)]
                            sp.dma_start(dst, part[2 * m + tile][p0:p0 + n, a, :]).then_inc(part_stored, 16)

                for m in range(2):
                    for tile in range(2):
                        store_part(m, tile)
                sp.wait_ge(v_read, ch * 2 + 2)
                for hq in range(QB):
                    sp.dma_start(V_v[bass.ds(b * QB + hq, 1), bass.ds(t, 1), :, :, :].rearrange("n t p s c -> p (n t) s c"),
                                 Vs[:, None, :, hq * G * DH:(hq + 1) * G * DH]).then_inc(v_stored, 16)
                sp.wait_ge(R_ready, ch + 2)
                sp.dma_start(R_v[bass.ds(ch, 1), :, :, :].rearrange("n p s c -> p n s c"), R[:, None, :, :])\
                    .then_inc(R_stored, 16)

            with sp.Fori(0, NCH // 2 - 1) as i2:
                for par in range(2):
                    body(i2 * 2 + par, par)
            load_qk(sp, scr, 0, w["Q0"], w["K0"], w["qk_loaded0"])
            for par in range(2):
                body(NCH - 2 + par, par)
            for k in range(2):
                sp.wait_ge(x_loaded[k], 16 * (NCH // 2 + 1))
            sp.wait_ge(v_stored, 16 + 16 * QB * NCH)
            sp.wait_ge(part_stored, 16 + 16 * STORES * NCH)
            sp.wait_ge(R_stored, 16 + 16 * NCH)

        @block.gpsimd
        def _(pool):
            me = Steps(pool, pool_steps, HC - 2)

            def rsqrt(out, in_):
                return pool.tensor_tensor(out=out[:, :], in0=in_[:, :], in1=w["mhalf"][:, :], op=ALU.pow)

            def add_constant(par, loaded):
                pool.wait_ge(x_loaded[par], loaded)
                pool.tensor_tensor(out=xc[par][:, :, :], in0=X[par][:, :, :],
                                   in1=w["CB"][:, None, :].to_broadcast([P, SUB, C]), op=ALU.add).then_inc(xc_ready, 1)

            add_constant(0, 16)
            pool.wait_ge(stats_ready, 1)
            rsqrt(rstd, ve).then_inc(rstd_ready, 1)
            with pool.Fori(0, NCH // 2) as i2:
                for par in range(2):
                    ch = i2 * 2 + par
                    me.start(ch)
                    for hc in range(1, HC):
                        if hc == 3:
                            pool.wait_ge(stats_ready, ch + 2)
                            rsqrt(rstd, ve).then_inc(rstd_ready, 1)
                        pool.wait_ge(g2_ready, ch * HC + hc + 1)
                        if hc > 1:
                            me.wait()
                        i = pool.tensor_tensor(out=gsum[:, :, :], in0=g[:, 0, :, :] if hc == 1 else gsum[:, :, :],
                                               in1=g[:, hc, :, :], op=ALU.add)
                        if hc < HC - 1:
                            me.done(i)
                    i.then_inc(gsum_ready, 1)
                    pool.wait_ge(R_ready, ch + 1)
                    add_constant(1 - par, i2 * 16 + 16 + 16 * par)
                    pool.wait_ge(fvar_ready, ch + 1)
                    rsqrt(frs, fve).then_inc(frs_ready, 1)
                    me.end()

        @block.vector
        def _(dve):
            me = Steps(dve, steps, 19)
            spare = dve.alloc_register("spare_of_dve")

            def stats(x, loaded, count):
                dve.wait_ge(loaded, count)
                for s in range(SUB):
                    i = dve.bn_stats(st6[:, s, :], x[:, s, :])
                me.done(i)
                wait_apart(dve, spare, steps, me.base + me.n, x_loaded[0], 16)
                for s in range(SUB):
                    i = dve.bn_aggr(mv[:, s, :], st6[:, s, :])
                me.done(i)
                me.wait()
                dve.tensor_scalar(ve[:, :], mv[:, :, 1], LN_EPS, None, ALU.add).then_inc(stats_ready, 1)

            def normalise(x, count):
                dve.wait_ge(rstd_ready, count)
                me.done(dve.scalar_tensor_tensor(out=nmr[:, :], in0=mv[:, :, 0], scalar=-1.0, in1=rstd[:, :],
                                                 op0=ALU.mult, op1=ALU.mult))
                me.wait()
                for s in range(SUB):
                    i = dve.tensor_scalar(xn[:, s, :], x[:, s, :], rstd[:, s:s + 1], nmr[:, s:s + 1],
                                          ALU.mult, ALU.add)
                i.then_inc(xn_ready, 1)

            def low_x(turn):
                dve.wait_ge(xT_ready, turn * (2 * CC) + 2 * CC)
                dve.tensor_tensor(out=xl[:, :, :], in0=xT[:, :, :], in1=xh[:, :, :], op=ALU.subtract)\
                    .then_inc(xl_ready, 1)

            def low_g(ch, hc):
                dve.wait_ge(gh_ready, ch * HC + hc + 1)
                dve.scalar_tensor_tensor(out=gl[:, hc, :], in0=g[:, hc, 0, :], scalar=w["lnw"][:, hc:hc + 1],
                                         in1=gh[:, hc, :], op0=ALU.mult, op1=ALU.subtract).then_inc(gl_ready, 1)

            def split_rest(dst, rest):
                me.done(dve.tensor_copy(dst[:, 1, :], rest[:, :]))
                me.wait()
                return dve.tensor_tensor(out=dst[:, 2, :], in0=rest[:, :], in1=dst[:, 1, :], op=ALU.subtract)

            def read_plain(m, ch):
                dve.wait_ge(part_stored, ch * (16 * STORES) + 16)
                dve.wait_ge(high_ready, ch * 2 + m + 1)
                dve.tensor_tensor(out=plain_rest[:, :], in0=bank[2 * m][:, :], in1=part[2 * m][:, 0, :], op=ALU.subtract)\
                    .then_inc(qk_read, 1)

            def split_plain(m, ch):
                dve.wait_ge(qk_read, ch * 4 + 2 * m + 1)
                split_rest(part[2 * m], plain_rest).then_inc(part_ready, 1)

            def read_rotated(m, ch, t):
                src = bank[2 * m + 1]
                dve.wait_ge(qk_ready, ch * 4 + 2 * m + 2)
                dve.tensor_tensor(out=rope[:, :], in0=src[:, :], in1=w["cos"][:, t], op=ALU.mult)
                for p0 in (0, 64):
                    i = dve.tensor_tensor(out=rot[64 - p0:128 - p0, :], in0=src[p0:p0 + 64, :],
                                          in1=w["sin"][p0:p0 + 64, t], op=ALU.mult)
                i.then_inc(qk_read, 1)

            def split_rotated(m, ch):
                dst = part[2 * m + 1]
                dve.wait_ge(qk_read, ch * 4 + 2 * m + 2)
                me.done(dve.tensor_tensor(out=rope[:, :], in0=rope[:, :], in1=rot[:, :], op=ALU.add))
                me.wait()
                me.done(dve.tensor_copy(dst[:, 0, :], rope[:, :]))
                me.wait()
                me.done(dve.tensor_tensor(out=rest[:, :], in0=rope[:, :], in1=dst[:, 0, :], op=ALU.subtract))
                me.wait()
                split_rest(dst, rest).then_inc(part_ready, 1)

            dve.memset(xn[:, 0, 0:1], 0.0).then_inc(ffn_read, 4)
            stats(X[0], x_loaded[0], 16)
            normalise(X[0], 1)
            low_x(0)
            first = me.n
            with dve.Fori(0, NCH // 2) as i2:
                for par in range(2):
                    ch = i2 * 2 + par
                    me.start(ch)
                    me.base = me.base + first
                    t = bass.ds((ch % TC) * CH, CH)
                    for hc in range(2):
                        low_g(ch, hc)
                    stats(X[1 - par], x_loaded[1 - par], i2 * 16 + 16 + 16 * par)
                    for hc in range(2, 5):
                        low_g(ch, hc)
                    dve.wait_ge(xT_in_psum, ch * 2 + 2)
                    normalise(X[1 - par], ch + 2)
                    low_g(ch, 5)
                    read_plain(0, ch)
                    low_g(ch, 6)
                    low_g(ch, 7)
                    read_rotated(0, ch, t)
                    split_plain(0, ch)
                    dve.wait_ge(part_ready, ch * 4 + 1)
                    read_plain(1, ch)
                    split_rotated(0, ch)
                    read_rotated(1, ch, t)
                    low_x(ch + 1)
                    split_plain(1, ch)
                    split_rotated(1, ch)
                    for s in range(SUB):
                        dve.wait_ge(ffn_ready, ch * 4 + s + 1)
                        me.done(dve.tensor_copy(fst[:, s, :], bank[s][:, C:C + 2]))
                        me.wait()
                        dve.scalar_tensor_tensor(out=ft[:, s, :], in0=w["NB"][:, :], scalar=fst[:, s, 0:1],
                                                 in1=bank[s][:, 0:C], op0=ALU.mult, op1=ALU.add).then_inc(ffn_read, 1)
                    me.done(dve.tensor_tensor(out=fmm[:, :], in0=fst[:, :, 0], in1=fst[:, :, 0], op=ALU.mult))
                    me.wait()
                    dve.scalar_tensor_tensor(out=fve[:, :], in0=fst[:, :, 1], scalar=LN_EPS, in1=fmm[:, :],
                                             op0=ALU.add, op1=ALU.subtract).then_inc(fvar_ready, 1)
                    dve.wait_ge(frs_ready, ch + 1)
                    me.done(dve.tensor_scalar(frw[:, :], frs[:, :], w["wmax"][:, 0:1], None, ALU.mult))
                    me.wait()
                    dve.wait_ge(ffn_read, ch * 4 + 8)
                    dve.wait_ge(xc_ready, ch + 1)
                    dve.wait_ge(R_stored, ch * 16 + 16)
                    for s in range(SUB):
                        i = dve.scalar_tensor_tensor(out=R[:, s, :], in0=ft[:, s, :], scalar=frw[:, s:s + 1],
                                                     in1=xc[par][:, s, :], op0=ALU.mult, op1=ALU.add)
                    i.then_inc(R_ready, 1)
                    me.end()

        @block.scalar
        def _(act):
            def xT_evac(turn):
                for cc in range(CC):
                    act.wait_ge(xT_in_psum, turn * 2 + cc + 1)
                    act.activation(xh[:, cc, :], bank[4 + cc][:, :], ACT.Copy).then_inc(xT_ready, 1)
                    act.activation(xT[:, cc, :], bank[4 + cc][:, :], ACT.Copy).then_inc(xT_ready, 1)

            def high(m, ch):
                act.wait_ge(part_stored, ch * (16 * STORES) + 16)
                act.wait_ge(qk_ready, ch * 4 + 2 * m + 1)
                act.activation(part[2 * m][:, 0, :], bank[2 * m][:, :], ACT.Copy).then_inc(high_ready, 1)

            xT_evac(0)
            with act.Fori(0, NCH) as ch:
                for hc in range(HC + 1):
                    if hc < HC:
                        act.wait_ge(h_ready, ch * HC + hc + 1)
                        act.activation(g[:, hc, 0, :], hidden_bank[hc % 4][:, :], ACT.Gelu).then_inc(h_read, 1)
                    if hc:
                        act.wait_ge(h_read, ch * HC + hc + 4)
                        act.activation(gh[:, hc - 1, :], g[:, hc - 1, 0, :], ACT.Copy, scale=w["lnw"][:, hc - 1:hc])\
                            .then_inc(gh_ready, 1)
                        act.activation(g[:, hc - 1, 1, :], g[:, hc - 1, 0, :], ACT.Square).then_inc(g2_ready, 1)
                    if hc == 6:
                        high(0, ch)
                high(1, ch)
                act.wait_ge(v_stored, ch * (16 * QB) + 16)
                for k in range(2):
                    act.wait_ge(v_ready, ch * 2 + k + 1)
                    act.activation(Vs[:, 2 * k:2 * k + 2, :], bank[4 + k][:, :].rearrange("p (s c) -> p s c", s=2),
                                   ACT.Copy).then_inc(v_read, 1)
                xT_evac(ch + 1)

        @block.tensor
        def _(pe):
            def transposes(turn):
                pe.wait_ge(xn_ready, turn + 1)
                for cc in range(CC):
                    for s in range(SUB):
                        i = pe.transpose(bank[4 + cc][:, s * P:(s + 1) * P], xn[:, s, cc * P:(cc + 1) * P], w["ident"][:, :])
                    i.then_inc(xT_in_psum, 1)

            def down_projection(ch, s):
                pe.wait_ge(qk_read, ch * 4 + s + 1)
                for hc in range(HC):
                    for k, x in enumerate((gh, gl)):
                        pe.matmul(bank[s][:, 0:C], lhsT=x[:, hc, s * P:(s + 1) * P], rhs=w["WP"][:, hc, :],
                                  start=hc + k == 0, stop=hc + k == HC)

            def hidden_means(s):
                for k in range(2):
                    i = pe.matmul(bank[s][:, C + k:C + k + 1], lhsT=gsum[:, k, s * P:(s + 1) * P], rhs=w["mean_col"][:, :],
                                  start=True, stop=True)
                i.then_inc(ffn_ready, 1)

            pe.matmul(bank[6][:, 0:1], lhsT=w["ident"][:, :], rhs=w["ident"][:, 0:1], start=True, stop=True)\
                .then_inc(h_read, 4)
            transposes(0)
            with pe.Fori(0, NCH) as ch:
                pe.wait_ge(xl_ready, ch + 1)
                for hc in range(HC):
                    pe.wait_ge(h_read, ch * HC + hc + 1)
                    for k, (cc, x) in enumerate(((0, xh), (1, xh), (0, xl), (1, xl))):
                        i = pe.matmul(hidden_bank[hc % 4][:, :], lhsT=w["WF"][:, cc, hc * P:(hc + 1) * P], rhs=x[:, cc, :],
                                      start=k == 0, stop=k == 3)
                    i.then_inc(h_ready, 1)
                for t in range(4):
                    pe.wait_ge(ffn_read, ch * 4 + t + 1)
                    for cc in range(CC):
                        i = pe.matmul(bank[t][:, :], lhsT=w["WQK"][:, cc, t * P:(t + 1) * P], rhs=xT[:, cc, :],
                                      start=cc == 0, stop=cc == CC - 1)
                    i.then_inc(qk_ready, 1)
                pe.wait_ge(h_read, (ch + 1) * HC + 4)
                for k in range(2):
                    for a in range(2):
                        s = 2 * k + a
                        for cc in range(CC):
                            i = pe.matmul(bank[4 + k][:, a * C:(a + 1) * C], lhsT=xT[:, cc, s * P:(s + 1) * P],
                                          rhs=w["WV"][:, cc, :], start=cc == 0, stop=cc == CC - 1)
                    i.then_inc(v_ready, 1)
                pe.wait_ge(gl_ready, ch * HC + HC)
                down_projection(ch, 0)
                down_projection(ch, 1)
                pe.wait_ge(v_read, ch * 2 + 2)
                transposes(ch + 1)
                down_projection(ch, 2)
                down_projection(ch, 3)
                pe.wait_ge(gsum_ready, ch + 1)
                for s in range(SUB):
                    hidden_means(s)



ST, SM, PT = 2, 3, 6
SLOTS = 3
UNITS = sum(2 * G * (c + 1) for c in range(TC))
PAIRS = UNITS // 2
DIAG = 2 * SUB * TC
BLOCKS = [(h, t, k) for h in range(G) for t in range(T // P) for k in range(t // SUB + 1)]
NB = len(BLOCKS)
QROWS = (0, 0, 0, 1, 1, 2)
KROWS = (0, 1, 2, 0, 1, 0)
KD = len(QROWS) * DH


LAG = 2
ORDER = [(c, j, CH - P * max(0, j - SUB * c)) for c in range(TC) for j in range(SUB * (c + 1))]


def block_width(g):
    h, t, k = BLOCKS[g]
    return P * (t % SUB + 1) if k == t // SUB else CH


def plan_blocks():
    steps = []
    for n in range(PAIRS + LAG):
        if n < PAIRS:
            steps += [2 * ORDER[n][2]] * 2
        if n >= LAG:
            steps += [4 * ORDER[n - LAG][2]]
    total = sum(steps)
    work = [block_width(g) + 64 for g in range(NB)]
    plan, seen, g = [], 0, HEAD
    done = sum(work[:g])
    for columns in steps:
        seen += columns
        share = min(1.0, AHEAD + (1 - AHEAD) * seen / (SPREAD * total)) * sum(work)
        now = []
        while g < NB and done + work[g] / 2 <= share:
            now.append(g)
            done += work[g]
            g += 1
        plan.append(now)
    assert g == NB
    return plan


SPREAD = 0.94
TRANSPOSE = PAIRS - 2
HEAD = SM
AHEAD = 0.015
PLAN = plan_blocks()


LOADS = 2 * len(QROWS)


def load_qk(sp, scr, quad, q, k, loaded):
    b, hq = quad // QB, quad % QB
    for name, dst, rows in (("Q", q, QROWS), ("K", k, KROWS)):
        for r, a in enumerate(rows):
            src = scr[name].rearrange("a b (q h e) t -> a b q e h t", h=G, e=DH)[a]
            if isinstance(quad, int):
                src = src[b, hq]
            else:
                src = src[bass.ds(b, 1), bass.ds(hq, 1), :, :, :].rearrange("b q e h t -> (b q e) h t")
            sp.dma_start(dst[r * DH:(r + 1) * DH, :, :], src).then_inc(loaded, 16)


def attention(nc, w, scr):
    with ExitStack() as ctx:
        def sb(name, shape, dt=fp32):
            return ctx.enter_context(nc.sbuf_tensor(name, shape, dt))

        def sem(name):
            return ctx.enter_context(nc.semaphore(name))

        Q = [w["Q0"]] + [sb(f"Q{i}", [KD + 2, G, T], bf16) for i in range(1, SLOTS)]
        K = [w["K0"]] + [sb(f"K{i}", [KD + 2, G, T], bf16) for i in range(1, SLOTS)]
        Vr = sb("V_raw", [P, T // P, G * DH])
        V = [sb(f"V{i}", [P, T // P, G, 2 * DH]) for i in range(SLOTS)]
        prob = [sb(f"prob{i}", [P, 2, CH]) for i in range(PT)]
        Y = sb("Y", [P, T])
        pm = sb("pm", [P, G, T // P, TC])
        ones = sb("ones_b", [P, 2 * G * T // P], bf16)
        m = sb("m", [P, P])
        mh = sb("mh", [G * T // P, P], bf16)
        ml = sb("ml", [G * T // P, P], bf16)
        mask = sb("mask", [P, CH], bf16)
        st = [ctx.enter_context(nc.psum_tensor(f"st{i}", [P, 2, CH], fp32)) for i in range(ST)]
        sm = [ctx.enter_context(nc.psum_tensor(f"sm{i}", [P, CH], fp32)) for i in range(SM)]
        pv = ctx.enter_context(nc.psum_tensor("pv", [P, CH], fp32))

        consts = sem("consts")
        pool_steps = sem("pool_steps")
        qk_loaded = [w["qk_loaded0"]] + [sem(f"qk_loaded{i}") for i in range(1, SLOTS)]
        ones_made = sem("ones_made")
        ones_placed = sem("ones_placed")
        v_loaded = sem("v_loaded")
        v_placed = sem("v_placed")
        st_ready = sem("st_ready")
        exp_done = sem("exp_done")
        masked = sem("masked")
        pair_used = sem("pair_used")
        pv_read = sem("pv_read")
        y_stored = sem("y_stored")
        sm_ready = sem("sm_ready")
        sm_read = sem("sm_read")
        m_ready = sem("m_ready")
        mrow_hi = sem("mrow_hi")
        m_loaded = sem("m_loaded")
        block = ctx.enter_context(nc.Block())

        YS = 2 * G
        order = ORDER
        diag = [j >= SUB * c for c, j, _ in order]

        def quads(eng, body):
            with eng.Fori(0, NQ // SLOTS) as it:
                for k in range(SLOTS):
                    body(it * SLOTS + k, k, False)
            body(NQ - 1, (NQ - 1) % SLOTS, True)

        @block.sync
        def _(sp):
            def load_v(quad):
                src = scr["V"].rearrange("n (j p) d -> n p j d", p=P)
                src = src[quad] if isinstance(quad, int) else \
                    src[bass.ds(quad, 1), :, :, :].rearrange("n p j d -> (n p) j d")
                sp.dma_start(Vr[:, :, :], src).then_inc(v_loaded, 16)

            def load_m(slot, count):
                sp.wait_ge(sm_read, count * (NB + 1) + SM)
                for r, src in enumerate((mh, ml)):
                    sp.dma_start(Q[slot][KD + r:KD + r + 1, :, :],
                                 src[:, :]).then_inc(m_loaded, 16)

            def body(quad, slot, last):
                if not last:
                    sp.wait_ge(pair_used, quad * PAIRS + PT // 2)
                    nxt = (slot + 2) % SLOTS
                    load_qk(sp, scr, (quad + 2) % NQ, Q[nxt], K[nxt], qk_loaded[nxt])
                    sp.wait_ge(v_placed, quad + 1)
                    load_v(quad + 1)
                    load_m((slot + 1) % SLOTS, quad + 2)
                sp.wait_ge(pv_read, quad * TC + TC + 1)
                for h in range(G):
                    row = quad * (G * DH) + h * DH
                    sp.dma_start(scr["Y"][bass.ds(row, DH), :], Y[2 * DH * h:2 * DH * h + DH, :]).then_inc(y_stored, 16)
                    sp.dma_start(scr["L"][bass.ds(quad * G + h, 1), :],
                                 Y[2 * DH * h + DH:2 * DH * h + DH + 1, :]).then_inc(y_stored, 16)

            grant(sp, (pv_read, 1), (y_stored, 16))
            load_v(0)
            sp.wait_ge(ones_made, 1)
            for s in range(SLOTS):
                sp.dma_start(K[s][KD:KD + 2, :, :], ones[:, :]).then_inc(ones_placed, 16)
            load_qk(sp, scr, 1, Q[1], K[1], qk_loaded[1])
            load_m(0, 1)
            quads(sp, body)
            sp.wait_ge(y_stored, 16 + 16 * YS * NQ)
            for s in range(SLOTS):
                sp.wait_ge(qk_loaded[s], 16 * LOADS * len([n for n in range(NQ + 1) if n % SLOTS == s]))

        @block.gpsimd
        def _(pool):
            spare = pool.alloc_register("spare_of_pool")
            pool.memset(ones[:, :], 1.0).then_inc(ones_made, 1)
            pool.memset(mask[:, :], 0.0).then_inc(pool_steps, 1)
            pool.wait_ge(pool_steps, 1)
            pool.affine_select(out=mask[:, CH - P:], in_=mask[:, CH - P:], compare_op=ALU.is_ge, fill=-1e30, base=0,
                               pattern=[[-1, P]], channel_multiplier=1).then_inc(consts, 1)

            def place_v(quad, slot):
                wait_apart(pool, spare, v_loaded, quad * 16 + 16, pool_steps, 1)
                pool.tensor_copy(V[slot][:, :, :, 0:DH], Vr[:, :, :].rearrange("p j (h d) -> p j h d", h=G))\
                    .then_inc(v_placed, 1)

            def body(quad, slot, last):
                d = 0
                for n, (c, j, width) in enumerate(order):
                    if n == 4 and not last:
                        place_v(quad + 1, (slot + 1) % SLOTS)
                    if not diag[n]:
                        continue
                    for u in (2 * n, 2 * n + 1):
                        x = prob[(slot * UNITS + u) % PT][:, :, 0:P]
                        wait_apart(pool, spare, exp_done, quad * UNITS + (u + 1 + ST), pool_steps, 1)
                        pool.affine_select(out=x, in_=x, compare_op=ALU.is_ge, fill=0.0, base=0,
                                           pattern=[[0, 2], [1, P]], channel_multiplier=-1).then_inc(masked, 1)
                        d += 1
                assert d == DIAG

            for s in range(SLOTS):
                pool.memset(V[s][:, :, :, DH:2 * DH], 1.0)
            place_v(0, 0)
            quads(pool, body)

        @block.scalar
        def _(act):
            def body(quad, slot, last):
                def evac(c):
                    ends = sum(x[0] <= c for x in order)
                    act.wait_ge(pair_used, quad * PAIRS + ends + PT // 2)
                    if c == 0:
                        act.wait_ge(y_stored, quad * (16 * YS) + 16)
                    act.activation(Y[:, c * CH:(c + 1) * CH], pv[:, :], ACT.Copy).then_inc(pv_read, 1)

                for n, (c, j, width) in enumerate(order):
                    act.wait_ge(pair_used, quad * PAIRS + n + 1)
                    for u in (2 * n, 2 * n + 1):
                        act.wait_ge(st_ready, quad * UNITS + u + 1)
                        act.activation(prob[(slot * UNITS + u) % PT][:, :, 0:width], st[u % ST][:, :, 0:width], ACT.Exp)\
                            .then_inc(exp_done, 1)
                    if n >= LAG and order[n - LAG][0] != order[n - LAG + 1][0]:
                        evac(order[n - LAG][0])
                evac(TC - 1)

            quads(act, body)

        @block.vector
        def _(dve):
            spare = dve.alloc_register("spare_of_dve_a")

            def block_max(g, base, ring):
                h, t, k = BLOCKS[g]
                width = P * (t % SUB + 1) if k == t // SUB else CH
                x = sm[(ring + g) % SM][:, 0:width]
                if k == t // SUB:
                    wait_apart(dve, spare, sm_ready, base + g + 1, consts, 1)
                    dve.tensor_tensor_reduce(x, x, mask[:, CH - width:], 1.0, -3e38, ALU.add, ALU.max,
                                             pm[:, h, t, k:k + 1]).then_inc(sm_read, 1)
                else:
                    dve.wait_ge(sm_ready, base + g + 1)
                    dve.tensor_reduce(out=pm[:, h, t, k:k + 1], in_=x, axis=AX.X, op=ALU.max).then_inc(sm_read, 1)

            def row_max(quad, base, ring):
                dve.wait_ge(sm_read, base + NB + SM)
                dve.tensor_reduce(out=m[:, 0:G * T // P], in_=pm[:, :, :, :].rearrange("p h t k -> p (h t) k"), axis=AX.X, op=ALU.max)\
                    .then_inc(m_ready, 1)
                x = sm[(ring + NB) % SM][0:G * T // P, 0:P]
                dve.wait_ge(sm_ready, base + NB + 1)
                if not isinstance(quad, int):
                    dve.wait_ge(m_loaded, quad * 32)
                dve.tensor_scalar(mh[:, :], x, -1.0, None, ALU.mult).then_inc(mrow_hi, 1)
                dve.wait_ge(mrow_hi, quad + 1)
                dve.scalar_tensor_tensor(out=ml[:, :], in0=x, scalar=-1.0, in1=mh[:, :], op0=ALU.mult, op1=ALU.subtract)\
                    .then_inc(sm_read, 1)

            def maxima(quad, slot):
                base, ring = quad * (NB + 1), slot * (NB + 1)
                for g in range(NB):
                    block_max(g, base, ring)
                row_max(quad, base, ring)

            dve.memset(m[:, :], 0.0)
            dve.memset(pm[:, :, :, :], -3e38).then_inc(sm_read, SM)
            maxima(0, 0)
            def body(quad, slot, last):
                if not last:
                    maxima(quad + 1, (slot + 1) % SLOTS)
            quads(dve, body)

        @block.tensor
        def _(pe):
            def scores_for_max(g, quad, slot):
                h, t, k = BLOCKS[g]
                width = block_width(g)
                dst = sm[(slot * (NB + 1) + g) % SM]
                pe.wait_ge(sm_read, quad * (NB + 1) + g + 1)
                pe.matmul(dst[:, 0:width], lhsT=Q[slot][0:KD, h, t * P:(t + 1) * P],
                          rhs=K[slot][0:KD, h, k * CH:k * CH + width], start=True, stop=True).then_inc(sm_ready, 1)

            def transpose_m(quad, slot):
                pe.wait_ge(sm_read, quad * (NB + 1) + NB + 1)
                pe.wait_ge(m_ready, quad + 1)
                pe.transpose(sm[(slot * (NB + 1) + NB) % SM][:, 0:P], m[:, :], w["ident"][:, :])\
                    .then_inc(sm_ready, 1)

            def scores(quad, slot, u):
                c, j, width = order[u // 2]
                pe.wait_ge(exp_done, quad * UNITS + u + 1)
                for a in range(2):
                    h = 2 * (u % 2) + a
                    i = pe.matmul(st[u % ST][:, a, 0:width], lhsT=K[slot][:, h, j * P:(j + 1) * P],
                                  rhs=Q[slot][:, h, (c + 1) * CH - width:(c + 1) * CH], start=True, stop=True)
                i.then_inc(st_ready, 1)

            def weighted_sums(quad, slot, n):
                c, j, width = order[n]
                if j == 0:
                    pe.wait_ge(pv_read, quad * TC + c + 1)
                if diag[n]:
                    pe.wait_ge(masked, quad * DIAG + 2 * sum(diag[:n + 1]))
                else:
                    pe.wait_ge(exp_done, quad * UNITS + 2 * n + 2 + ST)
                for h in range(G):
                    i = pe.matmul(pv[2 * DH * h:2 * DH * (h + 1), CH - width:CH], lhsT=V[slot][:, j, h, :],
                                  rhs=prob[(slot * UNITS + 2 * n + h // 2) % PT][:, h % 2, 0:width],
                                  start=j == 0, stop=j == SUB * (c + 1) - 1, tile_position=(0, 2 * DH * h))
                    if h == G - 1:
                        i.then_inc(pair_used, 1)

            pe.matmul(pv[:, 0:1], lhsT=w["ident"][:, :], rhs=w["ident"][:, 0:1], start=True, stop=True).then_inc(exp_done, ST)
            pe.matmul(pv[:, 0:1], lhsT=w["ident"][:, :], rhs=w["ident"][:, 0:1], start=True, stop=True).then_inc(pair_used, PT // 2)
            pe.wait_ge(qk_loaded[0], 16 * LOADS)
            for g in range(NB):
                scores_for_max(g, 0, 0)
            transpose_m(0, 0)
            pe.wait_ge(ones_placed, 16 * SLOTS)

            def body(quad, slot, last):
                if not last:
                    turn = quad // SLOTS
                    nxt = (slot + 1) % SLOTS
                    pe.wait_ge(qk_loaded[nxt], (turn + (2 if nxt == 0 else 1)) * (16 * LOADS))
                    for g in range(HEAD):
                        scores_for_max(g, quad + 1, nxt)
                pe.wait_ge(m_loaded, quad * 32 + 32)
                pe.wait_ge(v_placed, quad + 1)
                plan = iter(PLAN)

                def next_blocks():
                    for g in () if last else next(plan):
                        scores_for_max(g, quad + 1, nxt)

                for n in range(PAIRS + LAG):
                    for u in (2 * n, 2 * n + 1) if n < PAIRS else ():
                        scores(quad, slot, u)
                        next_blocks()
                    if not last and n == TRANSPOSE:
                        transpose_m(quad + 1, nxt)
                    if n >= LAG:
                        weighted_sums(quad, slot, n - LAG)
                        next_blocks()

            quads(pe, body)


BUFS = 4


def project_out(nc, io, w, scr):
    with ExitStack() as ctx:
        def sb(name, shape, dt=fp32):
            return ctx.enter_context(nc.sbuf_tensor(name, shape, dt))

        def sem(name):
            return ctx.enter_context(nc.semaphore(name))

        Wc = sb("Wc", [P, CC, C])
        ones = sb("ones16", [H, CC, H // CC, DH])
        E = sb("E", [H, CC, H // CC, DH])
        Y = [sb(f"Yt{i}", [P, CC, CH]) for i in range(BUFS)]
        sums = [sb(f"sums{i}", [H, CH]) for i in range(BUFS)]
        rl = [sb(f"rl{i}", [H, CH]) for i in range(BUFS)]
        Yn = [sb(f"Yn{i}", [P, CC, CH]) for i in range(BUFS)]
        R = [sb(f"Rt{i}", [P, SUB, C]) for i in range(BUFS)]
        out = [sb(f"out{i}", [P, SUB, C]) for i in range(BUFS)]
        pr = [ctx.enter_context(nc.psum_tensor(f"pr{i}", [P, CH], fp32)) for i in range(4)]
        po = [ctx.enter_context(nc.psum_tensor(f"po{i}", [P, 2, C], fp32)) for i in range(4)]
        wc_loaded = sem("wc_loaded")
        e_ready = sem("e_ready")
        sums_loaded = [sem(f"sums_loaded{i}") for i in range(BUFS)]
        in_loaded = [sem(f"in_loaded{i}") for i in range(BUFS)]
        inverted = sem("inverted")
        spread = sem("spread")
        normed = sem("normed")
        projected = sem("projected")
        added = sem("added")
        out_stored = [sem(f"out_stored{i}") for i in range(BUFS)]
        block = ctx.enter_context(nc.Block())
        R_v = scr["R"].rearrange("(n s p) c -> n p s c", p=P, s=SUB)
        O_v = io["out"].rearrange("(n s p) c -> n p s c", p=P, s=SUB)
        Y_v = scr["Y"].rearrange("(b a p) (t q) -> b t p a q", p=P, a=CC, q=CH)
        L_v = scr["L"].rearrange("(b h) (t q) -> b t h q", h=H, q=CH)

        def chunks(eng, body):
            with eng.Fori(0, NCH // BUFS) as turn:
                for k in range(BUFS):
                    body(turn, turn * BUFS + k, k)

        @block.sync
        def _(sp):
            grant(sp, (added, 2 * BUFS), *((s, 16) for s in out_stored))

            def body(b, ch, t):
                sp.wait_ge(added, ch * 2 + 2)
                sp.dma_start(sums[t][:, None, :], L_v[bass.ds(b, 1), t, :, :].rearrange("b h q -> h b q"))\
                    .then_inc(sums_loaded[t], 16)
                sp.dma_start(Y[t][:, None, :, :], Y_v[bass.ds(b, 1), t, :, :, :].rearrange("b p a q -> p b a q"))\
                    .then_inc(in_loaded[t], 16)
                sp.dma_start(R[t][:, None, :, :], R_v[bass.ds(ch, 1), :, :, :].rearrange("n p s c -> p n s c"))\
                    .then_inc(in_loaded[t], 16)

            chunks(sp, body)

        @block.gpsimd
        def _(pool):
            pool.memset(ones[:, :, :, :], 1.0).then_inc(e_ready, 1)
            pool.wait_ge(e_ready, 1)
            pool.affine_select(out=E[:, :, :, :], in_=ones[:, :, :, :], compare_op=ALU.is_equal, fill=0.0, base=0,
                               pattern=[[-(H // CC), CC], [-1, H // CC], [0, DH]], channel_multiplier=1).then_inc(e_ready, 1)

        @block.vector
        def _(dve):
            def invert(turn, k):
                turn, k = turn + k // BUFS, k % BUFS
                dve.wait_ge(sums_loaded[k], turn * 16 + 16)
                dve.reciprocal(rl[k][:, :], sums[k][:, :]).then_inc(inverted, 1)

            def normalise(turn, ch, k):
                turn, k = turn + k // BUFS, k % BUFS
                dve.wait_ge(in_loaded[k], turn * 32 + 32)
                for a in range(CC):
                    dve.wait_ge(spread, ch * 2 + a + 1)
                    dve.tensor_tensor(out=Yn[k][:, a, :], in0=Y[k][:, a, :], in1=pr[2 * (k % 2) + a][:, :], op=ALU.mult)\
                        .then_inc(normed, 1)

            def add(turn, ch, k):
                dve.wait_ge(out_stored[k], turn * 16 + 16)
                for j in range(2):
                    dve.wait_ge(projected, ch * 2 + j + 1)
                    dve.tensor_tensor(out=out[k][:, 2 * j:2 * j + 2, :], in0=R[k][:, 2 * j:2 * j + 2, :],
                                      in1=po[2 * (k % 2) + j][:, :, :], op=ALU.add).then_inc(added, 1)

            def body(turn, ch, k, left=BUFS):
                if left >= 1:
                    normalise(turn, ch + 1, k + 1)
                if left >= 2:
                    invert(turn, k + 2)
                add(turn, ch, k)

            invert(0, 0)
            normalise(0, 0, 0)
            invert(0, 1)
            with dve.Fori(0, NCH // BUFS - 1) as turn:
                for k in range(BUFS):
                    body(turn, turn * BUFS + k, k)
            for k in range(BUFS):
                body(NCH // BUFS - 1, NCH - BUFS + k, k, BUFS - 1 - k)

        @block.scalar
        def _(act):
            def body(turn, ch, k):
                act.wait_ge(added, ch * 2 + 2 * BUFS + 2)
                act.dma_start(O_v[bass.ds(ch, 1), :, :, :].rearrange("n p s c -> p n s c"), out[k][:, None, :, :])\
                    .then_inc(out_stored[k], 16)

            act.dma_start(Wc[:, :, :], io["Wc"].rearrange("(a p) c -> p a c", p=P)).then_inc(wc_loaded, 16)
            chunks(act, body)
            for k in range(BUFS):
                act.wait_ge(out_stored[k], 16 + 16 * (NCH // BUFS))

        @block.tensor
        def _(pe):
            def spread_out(ch, k):
                pe.wait_ge(inverted, ch + 1)
                for a in range(CC):
                    pe.matmul(pr[2 * (k % 2) + a][:, :], lhsT=E[:, a, :, :].rearrange("k h d -> k (h d)"), rhs=rl[k][:, :],
                              start=True, stop=True).then_inc(spread, 1)

            def body(ch, k, last=False):
                if not last:
                    spread_out(ch + 1, (k + 1) % BUFS)
                pe.wait_ge(normed, ch * 2 + 2)
                for j in range(2):
                    for s in range(2):
                        for a in range(CC):
                            i = pe.matmul(po[2 * (k % 2) + j][:, s, :], lhsT=Yn[k][:, a, (2 * j + s) * P:(2 * j + s + 1) * P],
                                          rhs=Wc[:, a, :], start=a == 0, stop=a == CC - 1)
                    i.then_inc(projected, 1)

            pe.wait_ge(e_ready, 2)
            spread_out(0, 0)
            pe.wait_ge(wc_loaded, 16)
            with pe.Fori(0, NCH // BUFS - 1) as turn:
                for k in range(BUFS):
                    body(turn * BUFS + k, k)
            for k in range(BUFS):
                body(NCH - BUFS + k, k, k == BUFS - 1)


def build(nc, io):
    scr = {
        "Q": nc.dram_tensor("scratch_q", (PARTS, B, H * DH, T), bf16).ap(),
        "K": nc.dram_tensor("scratch_k", (PARTS, B, H * DH, T), bf16).ap(),
        "V": nc.dram_tensor("scratch_v", (NQ, T, G * DH), fp32).ap(),
        "R": nc.dram_tensor("scratch_r", (B * T, C), fp32).ap(),
        "Y": nc.dram_tensor("scratch_y", (B * H * DH, T), fp32).ap(),
        "L": nc.dram_tensor("scratch_l", (B * H, T), fp32).ap(),
    }
    with ExitStack() as ctx:
        w = {"ident": ctx.enter_context(nc.sbuf_tensor("ident", [P, P], fp32)),
             "Q0": ctx.enter_context(nc.sbuf_tensor("Q0", [KD + 2, G, T], bf16)),
             "K0": ctx.enter_context(nc.sbuf_tensor("K0", [KD + 2, G, T], bf16)),
             "qk_loaded0": ctx.enter_context(nc.semaphore("qk_loaded0"))}
        with ExitStack() as early:
            for name, shape, dt in (("mhalf", [P, SUB], fp32), ("mean_col", [P, 1], fp32), ("WQK", [P, CC, 4 * P], fp32),
                                    ("lnw", [P, HC], fp32), ("wmax", [P, 1], fp32), ("wall", [P, 1], fp32),
                                    ("WV", [P, CC, C], fp32), ("WF", [P, CC, HID], fp16), ("WP", [P, HC, C], fp16),
                                    ("NB", [P, C], fp32), ("CB", [P, C], fp32), ("cos", [P, T], fp32), ("sin", [P, T], fp32)):
                w[name] = early.enter_context(nc.sbuf_tensor("w" + name, shape, dt))
            w["X"] = [early.enter_context(nc.sbuf_tensor(f"x{i}", [P, SUB, C], fp32)) for i in range(2)]
            w["x_loaded"] = [early.enter_context(nc.semaphore(f"x_loaded{i}")) for i in range(2)]
            make_weights(nc, io, w)
            project_and_feed_forward(nc, io, w, scr)
        attention(nc, w, scr)
        project_out(nc, io, w, scr)


_INS = {"x": "L0_attn_x", "Wq_down": "L0_attn_Wq_down", "Wk_down": "L0_attn_Wk_down", "Wv_down": "L0_attn_Wv_down",
        "Wq_up_c": "L0_attn_Wq_up_c", "Wq_up_e": "L0_attn_Wq_up_e", "Wk_up_c": "L0_attn_Wk_up_c",
        "Wk_up_e": "L0_attn_Wk_up_e", "Wv_up": "L0_attn_Wv_up", "Wc": "L0_attn_Wc", "W_fc": "L0_ffn_W_fc",
        "ln_w": "L0_ffn_ln_w", "ln_b": "L0_ffn_ln_b", "W_proj": "L0_ffn_W_proj"}


def _rope_tables():
    import numpy as np
    half = DH // 2
    inv = (1.0 / np.float32(10000.0) ** (np.arange(0, half, 2, dtype=np.float32) / np.float32(half))).astype(np.float32)
    emb = np.concatenate([np.arange(T, dtype=np.float32)[:, None] * inv] * 2, axis=-1)
    dim = np.array([2 * (r % 4) + r // 64 for r in range(P)])
    cos, sin = [f(emb)[:, dim].T.astype(np.float32) for f in (np.cos, np.sin)]
    return np.ascontiguousarray(cos), np.concatenate([sin[64:], -sin[:64]])


def kernel(**inputs):
    import numpy as _np
    import concourse.bacc as _bacc
    from concourse import mybir as _mybir
    from concourse.bass_utils import run_bass_kernel_spmd as _run

    nc = _bacc.Bacc("TRN2", target_bir_lowering=False, num_devices=1)
    arrays, io = {}, {}
    for short, name in _INS.items():
        arrays[f"in_{short}"] = _np.ascontiguousarray(inputs[name])
    shape = arrays["in_x"].shape
    arrays["in_x"] = arrays["in_x"].reshape(-1, shape[-1])
    arrays["in_cos"], arrays["in_sin"] = _rope_tables()
    for name, a in arrays.items():
        io[name[3:]] = nc.dram_tensor(name, a.shape, _mybir.dt.from_np(a.dtype), kind="ExternalInput").ap()
    io["out"] = nc.dram_tensor("out_0", arrays["in_x"].shape, _mybir.dt.float32, kind="ExternalOutput").ap()
    build(nc, io)
    r = _run(nc, [arrays], core_ids=[0])
    return r.results[0]["out_0"].reshape(shape)
```
